# Optimizing a Trainium2 kernel written in Bass

```python
import numpy as np
import jax
import jax.numpy as jnp

def _softmax(x, axis=-1):
    return jax.nn.softmax(x, axis=axis)

def _gelu(x):
    return jax.nn.gelu(x, approximate=True)

def _silu(x):
    return jax.nn.silu(x)

def _sigmoid(x):
    return jax.nn.sigmoid(x)

def _layernorm(x, axis=-1, eps=1e-05):
    m = jnp.mean(x, axis=axis, keepdims=True)
    v = jnp.var(x, axis=axis, keepdims=True)
    return (x - m) / jnp.sqrt(v + eps)

def _scatter_add(tgt, idx, src, axis=0):
    return tgt.at[idx].add(src)

def _segment_sum(src, seg, n):
    return jax.ops.segment_sum(src, seg, n)
kernel_name = 'mk_decoder_postln_d1_seqx_r8_23a7bd'

def setup_inputs(seed: int=0):
    np.random.seed(seed)
    _w = jnp.asarray

    def _rec_inputs():
        import jax
        import jax.numpy as jnp
        _rk = jax.random.key(seed)
        x = -0.0003929 + 0.9999 * jax.random.normal(jax.random.fold_in(_rk, 1), (32, 128, 128), jnp.float32)
        _lenS = 128 - jax.random.randint(jax.random.fold_in(_rk, 7), (32,), 0, max(1, 128 // 4) + 1, jnp.int32)
        _lenS2 = 128 - jax.random.randint(jax.random.fold_in(_rk, 8), (32,), 0, max(1, 128 // 4) + 1, jnp.int32)
        _ctx_1024P = jax.random.normal(jax.random.fold_in(_rk, 11), (32, 16, 128), jnp.float32)
        _ctx_1024c = jax.random.dirichlet(jax.random.fold_in(_rk, 511), 0.3 * jnp.ones((16,), jnp.float32), (32, 128))
        _ctx_1024t = jnp.einsum('bsk,bkd->bsd', _ctx_1024c, _ctx_1024P)
        _ctx_1024t = _ctx_1024t * jax.lax.rsqrt(jnp.mean(jnp.square(_ctx_1024t)) + 1e-12) * 0.953939
        ctx_1024 = 2.81802e-05 + 1.00001 * (_ctx_1024t + 0.3 * jax.random.normal(jax.random.fold_in(_rk, 611), (32, 128, 128), jnp.float32))
        return (x, ctx_1024)
    x, ctx_1024 = _rec_inputs()

    def _L0_attn_setup():
        import jax, jax.numpy as jnp
        import numpy as np
        B, N, EMBED, HEADS = (1, 256, 128, 16)
        HD = EMBED // HEADS
        BASE = 10000.0
        EPS = 1e-05

        def _rope(t):
            d = t.shape[-1]
            n = t.shape[-2]
            inv_freq = 1.0 / BASE ** (jnp.arange(0, d, 2, dtype=jnp.float32) / d)
            pos = jnp.arange(n, dtype=jnp.float32)
            ang = pos[:, None] * inv_freq[None, :]
            cos = jnp.concatenate([jnp.cos(ang), jnp.cos(ang)], axis=-1)
            sin = jnp.concatenate([jnp.sin(ang), jnp.sin(ang)], axis=-1)
            t1, t2 = (t[..., :d // 2], t[..., d // 2:])
            rot = jnp.concatenate([-t2, t1], axis=-1)
            return t * cos + rot * sin
        key = jax.random.key(seed)
        ks = jax.random.split(key, 7)
        s = EMBED ** (-0.5)
        return {'x': jax.random.normal(ks[0], (B, N, EMBED), dtype=jnp.float32), 'Wq': jax.random.normal(ks[1], (EMBED, EMBED), dtype=jnp.float32) * s, 'Wk': jax.random.normal(ks[2], (EMBED, EMBED), dtype=jnp.float32) * s, 'Wv': jax.random.normal(ks[3], (EMBED, EMBED), dtype=jnp.float32) * s, 'Wo': jax.random.normal(ks[4], (EMBED, EMBED), dtype=jnp.float32) * s, 'Wg1': jax.random.normal(ks[5], (EMBED, HD), dtype=jnp.float32) * s, 'Wg2': jax.random.normal(ks[6], (HD, EMBED), dtype=jnp.float32) * HD ** (-0.5), 'ln_w': jnp.ones((EMBED,), dtype=jnp.float32), 'ln_b': jnp.zeros((EMBED,), dtype=jnp.float32)}
    _L0_attn_all = _L0_attn_setup()
    _L0_attn_in = {k: v for k, v in _L0_attn_all.items() if k in ('Wq', 'Wk', 'Wv', 'Wo', 'Wg1', 'Wg2', 'ln_w', 'ln_b')}
    del _L0_attn_all

    def _L0_xattn_setup():
        import jax, jax.numpy as jnp
        import numpy as np
        B, T, D = (8, 256, 128)
        key = jax.random.key(seed)
        k1, k2, k3, k4 = jax.random.split(key, 4)
        k = jax.random.normal(k1, (B, T, D), dtype=jnp.float32)
        v = jax.random.normal(k2, (B, T, D), dtype=jnp.float32)
        w = jax.random.uniform(k3, (D,), dtype=jnp.float32, minval=0.0005, maxval=0.008)
        u = 0.1 * jax.random.normal(k4, (D,), dtype=jnp.float32)
        return {'k': k, 'v': v, 'w': w, 'u': u}
    _L0_xattn_all = _L0_xattn_setup()
    _L0_xattn_in = {k: v for k, v in _L0_xattn_all.items() if k in ('w', 'u')}
    del _L0_xattn_all

    def _L0_ffn_setup():
        import jax, jax.numpy as jnp
        import numpy as np
        NUM_EXPERTS = 160
        TOP_K = 8
        ROUTED_SCALE = 2.5
        HIDDEN = 128
        INTER = 64
        key = jax.random.key(seed)
        ks = jax.random.split(key, 7)
        B, S = (1, 256)
        return {'hidden_states': jax.random.normal(ks[0], (B, S, HIDDEN), dtype=jnp.float32), 'router_w': jax.random.normal(ks[1], (NUM_EXPERTS, HIDDEN), dtype=jnp.float32) * 0.02, 'expert_bias': jnp.zeros((NUM_EXPERTS,), dtype=jnp.float32), 'w_gate': jax.random.normal(ks[2], (NUM_EXPERTS, INTER, HIDDEN), dtype=jnp.float32) * 0.02, 'w_down': jax.random.normal(ks[3], (NUM_EXPERTS, HIDDEN, INTER), dtype=jnp.float32) * 0.02, 'w_gate_shared': jax.random.normal(ks[4], (INTER, HIDDEN), dtype=jnp.float32) * 0.02, 'w_down_shared': jax.random.normal(ks[5], (HIDDEN, INTER), dtype=jnp.float32) * 0.02}
    _L0_ffn_all = _L0_ffn_setup()
    _L0_ffn_in = {k: v for k, v in _L0_ffn_all.items() if k in ('router_w', 'expert_bias', 'w_gate', 'w_down', 'w_gate_shared', 'w_down_shared')}
    del _L0_ffn_all
    return {'x': x, 'ctx_1024': ctx_1024, 'L0_attn_Wq': _L0_attn_in['Wq'], 'L0_attn_Wk': _L0_attn_in['Wk'], 'L0_attn_Wv': _L0_attn_in['Wv'], 'L0_attn_Wo': _L0_attn_in['Wo'], 'L0_attn_Wg1': _L0_attn_in['Wg1'], 'L0_attn_Wg2': _L0_attn_in['Wg2'], 'L0_attn_ln_w': _L0_attn_in['ln_w'], 'L0_attn_ln_b': _L0_attn_in['ln_b'], 'L0_xattn_w': _L0_xattn_in['w'], 'L0_xattn_u': _L0_xattn_in['u'], 'L0_ffn_router_w': _L0_ffn_in['router_w'], 'L0_ffn_expert_bias': _L0_ffn_in['expert_bias'], 'L0_ffn_w_gate': _L0_ffn_in['w_gate'], 'L0_ffn_w_down': _L0_ffn_in['w_down'], 'L0_ffn_w_gate_shared': _L0_ffn_in['w_gate_shared'], 'L0_ffn_w_down_shared': _L0_ffn_in['w_down_shared']}

def reference(x, ctx_1024, L0_attn_Wq, L0_attn_Wk, L0_attn_Wv, L0_attn_Wo, L0_attn_Wg1, L0_attn_Wg2, L0_attn_ln_w, L0_attn_ln_b, L0_xattn_w, L0_xattn_u, L0_ffn_router_w, L0_ffn_expert_bias, L0_ffn_w_gate, L0_ffn_w_down, L0_ffn_w_gate_shared, L0_ffn_w_down_shared):
    import jax
    import jax.numpy as jnp

    def _L0_attn_ref(x, Wq, Wk, Wv, Wo, Wg1, Wg2, ln_w, ln_b):
        import jax, jax.numpy as jnp
        import numpy as np
        B, N, EMBED, HEADS = (1, 256, 128, 16)
        HD = EMBED // HEADS
        BASE = 10000.0
        EPS = 1e-05

        def _rope(t):
            d = t.shape[-1]
            n = t.shape[-2]
            inv_freq = 1.0 / BASE ** (jnp.arange(0, d, 2, dtype=jnp.float32) / d)
            pos = jnp.arange(n, dtype=jnp.float32)
            ang = pos[:, None] * inv_freq[None, :]
            cos = jnp.concatenate([jnp.cos(ang), jnp.cos(ang)], axis=-1)
            sin = jnp.concatenate([jnp.sin(ang), jnp.sin(ang)], axis=-1)
            t1, t2 = (t[..., :d // 2], t[..., d // 2:])
            rot = jnp.concatenate([-t2, t1], axis=-1)
            return t * cos + rot * sin
        b, n, _ = x.shape
        q = jax.nn.silu(x @ Wq)
        k = jax.nn.silu(x @ Wk)
        v = x @ Wv
        split = lambda t: t.reshape(b, n, HEADS, HD).transpose(0, 2, 1, 3)
        q, k, v = (split(q), split(k), split(v))
        q = _rope(q)
        k = _rope(k)
        energy = jnp.einsum('bhnd,bhmd->bhnm', q, k)
        mask = jnp.tril(jnp.ones((n, n), dtype=energy.dtype))
        energy = energy * mask
        out = jnp.einsum('bhnm,bhmd->bhnd', energy, v)
        out = out.transpose(0, 2, 1, 3).reshape(b, n, EMBED)
        gate = jax.nn.sigmoid(x @ Wg1 @ Wg2)
        out = out * gate
        mu = out.mean(axis=-1, keepdims=True)
        var = ((out - mu) ** 2).mean(axis=-1, keepdims=True)
        out = (out - mu) / jnp.sqrt(var + EPS) * ln_w + ln_b
        return out @ Wo

    def _L0_xattn_ref(k, v, w, u):
        import jax, jax.numpy as jnp
        import numpy as np
        B, T, D = (8, 256, 128)
        Tn = k.shape[-2]
        kt = jnp.moveaxis(k, -2, 0)
        vt = jnp.moveaxis(v, -2, 0)
        ed = jnp.exp(-w)
        eg = jnp.exp(w)

        def step(carry, xs):
            A, Bm = carry
            kk, vv, t = xs
            out = A + jnp.exp(u + kk) * (vv * Bm + jnp.maximum(t - 1.0, 0.0))
            inc = jnp.where(t == 0.0, 0.0, 1.0)
            A = ed * A + inc * jnp.exp(kk) * vv
            Bm = eg * Bm + inc * jnp.exp(-kk)
            return ((A, Bm), out)
        A0 = jnp.zeros_like(kt[0])
        B0 = jnp.zeros_like(kt[0])
        ts = jnp.arange(Tn, dtype=k.dtype)
        (_, _), out = jax.lax.scan(step, (A0, B0), (kt, vt, ts))
        return jnp.moveaxis(out, 0, -2)

    def _L0_ffn_ref(hidden_states, router_w, expert_bias, w_gate, w_down, w_gate_shared, w_down_shared):
        import jax, jax.numpy as jnp
        import numpy as np
        NUM_EXPERTS = 160
        TOP_K = 8
        ROUTED_SCALE = 2.5
        HIDDEN = 128
        INTER = 64
        B, S, H = hidden_states.shape
        x = hidden_states.reshape(-1, H)
        T = x.shape[0]
        logits = x @ router_w.T + expert_bias[None, :]
        probs = jax.nn.sigmoid(logits)
        top_w, top_idx = jax.lax.top_k(probs, TOP_K)
        top_w = top_w / (jnp.sum(top_w, axis=-1, keepdims=True) + 1e-09)
        top_w = top_w * ROUTED_SCALE
        combine = jnp.zeros((T, NUM_EXPERTS), dtype=x.dtype)
        combine = combine.at[jnp.arange(T)[:, None], top_idx].set(top_w)
        h1 = jax.nn.silu(jnp.einsum('th,eih->eti', x, w_gate))
        h1w = h1 * combine.T[:, :, None]
        routed = jnp.einsum('eti,ehi->th', h1w, w_down)
        shared = jax.nn.silu(x @ w_gate_shared.T) @ w_down_shared.T
        return (routed + shared).reshape(B, S, H)
    x = _layernorm(x + _L0_attn_ref(x, L0_attn_Wq, L0_attn_Wk, L0_attn_Wv, L0_attn_Wo, L0_attn_Wg1, L0_attn_Wg2, L0_attn_ln_w, L0_attn_ln_b), axis=-1)
    x = _layernorm(x + _L0_xattn_ref(x, ctx_1024, L0_xattn_w, L0_xattn_u), axis=-1)
    x = _layernorm(x + _L0_ffn_ref(x, L0_ffn_router_w, L0_ffn_expert_bias, L0_ffn_w_gate, L0_ffn_w_down, L0_ffn_w_gate_shared, L0_ffn_w_down_shared), axis=-1)
    return x

_drawn_inputs = setup_inputs


def setup_inputs(seed=0):
    import zlib

    import numpy as np

    out = dict(_drawn_inputs(seed))
    spreads = {'L0_attn_ln_w': (1.0, 0.2), 'L0_attn_ln_b': (0.0, 0.1), 'L0_ffn_expert_bias': (0.0, 0.578)}
    factors = {'L0_ffn_router_w': 3.68,
     'L0_ffn_w_gate': 3.506,
     'L0_ffn_w_down': 3.479,
     'L0_ffn_w_gate_shared': 3.042,
     'L0_ffn_w_down_shared': 2.949}
    for name, (base, spread) in spreads.items():
        noise = np.random.default_rng([zlib.crc32(name.encode()), seed]).standard_normal(out[name].shape)
        drawn = base * np.exp(spread * noise) if base else spread * noise
        out[name] = jnp.asarray(drawn.astype(out[name].dtype))
    for name, factor in factors.items():
        out[name] = (out[name] * factor).astype(out[name].dtype)
    return out
```

```python
from contextlib import ExitStack

import numpy as np
import concourse.bass as bass
from concourse import mybir

ALU = mybir.AluOpType
ACT = mybir.ActivationFunctionType
F32 = mybir.dt.float32
F32R = mybir.dt.float32r
BF16 = mybir.dt.bfloat16
I32 = mybir.dt.int32

P = 128
SEQ = 128
BT = 4
N = SEQ * BT
HALF = 64
HD = 8
NR, NJ = 4, 4
NE, INTER = 160, 64
PAIRS = NE // 2
STEPS = PAIRS + 1
LAG = 4
CH = 4
NCH = PAIRS // CH
SLOTS = 4
GE = 32
NG = NE // GE
EPS = 1e-5
MAGIC = 0x5F3759DF
HSLOTS = 6
PROJECT_AT = (7, 8, 10, 11)
ENERGY_AT = (23, 26, 31, 34)
HEADS_AT = (29, 37)
CHAIN = 59
OUT_CHAIN = 14


class Tile:

    def __init__(self, it, base):
        self.it, self.base = it, base

    def at(self, k, more=0):
        if self.it is None:
            return self.base * k + more
        return self.it * (2 * k) + (self.base * k + more)

    def after(self, n):
        return Tile(self.it, self.base + n)

    @property
    def par(self):
        return self.base % 2


def wait(eng, sem, value):
    if not isinstance(value, int) or value > 0:
        eng.wait_ge(sem, value)


def build_program(nc, xT, xtok, cT, wqkv, wg1T, wg2, wo, lnw, lnb, wx, ux, rw, rbias, wgs, wds,
                  experts, cosT, sinT, cmask, bdmask, ident, center, hmask, sel, tm1, out):
    tokens = xT.shape[1]
    TILES = tokens // N
    LOOPS = (TILES - 2) // 2
    assert TILES == 2 * LOOPS + 2

    with ExitStack() as ctx:
        def sb(name, shape, dt=F32):
            return ctx.enter_context(nc.sbuf_tensor(name, shape, dt))

        def sem(name):
            return ctx.enter_context(nc.semaphore(name))

        scratch = nc.dram_tensor("split_experts", [P, PAIRS, 4, P], F32, kind="Internal").ap()

        wqkv_s = sb("wqkv_s", [P, 3 * P])
        wg1_s, wg2_s = sb("wg1_s", [HD, P]), sb("wg2_s", [HD, P])
        wg_s = sb("wg_s", [P, P])
        wo_s, wow_s = sb("wo_s", [P, P]), sb("wow_s", [P, P])
        wc_s = sb("wc_s", [P, 2, P])
        lnb_wide, attn_bias = sb("lnb_wide", [P, P]), sb("attn_bias", [P, P])
        cols = sb("cols", [P, 8])
        cos_s, sin_s = sb("cos_s", [P, 2 * P]), sb("sin_s", [P, 2 * P])
        cmask_s, bd_s = sb("cmask_s", [P, HALF]), sb("bd_s", [P, P])
        ident_s, identb = sb("ident_s", [P, P]), sb("identb", [P, P], BF16)
        hmask_s = sb("hmask_s", [P, NR])
        sel_s = sb("sel_s", [3 * GE, 16, P], BF16)
        decay_a, decay_b = sb("decay_a", [P, BT, SEQ]), sb("decay_b", [P, BT, SEQ])
        tm1_s = sb("tm1_s", [P, SEQ])
        rw_f, rwh, rwl = sb("rw_f", [P, NE]), sb("rwh", [P, NE], F32R), sb("rwl", [P, NE], F32R)
        rbias_s = sb("rbias_s", [P, NE])
        wgs_f, wgsh, wgsl = sb("wgs_f", [P, INTER]), sb("wgsh", [P, INTER], F32R), sb("wgsl", [P, INTER], F32R)
        wds_f, wdsh, wdsl = sb("wds_f", [INTER, P]), sb("wdsh", [INTER, P], F32R), sb("wdsl", [INTER, P], F32R)
        ring = sb("ring", [P, SLOTS, CH, 4, P], F32R)

        raw = sb("raw", [P, 2, CH, 2, P])

        xT_s, xtok_s, cT_s = sb("xT_s", [P, N]), sb("xtok_s", [P, BT, P]), sb("cT_s", [P, BT, SEQ])
        qk = sb("qk", [P, BT, 2 * P])
        qkr = sb("qkr", [P, BT, 2 * P])
        v_tok = sb("v_tok", [P, BT, P])
        v_head = sb("v_head", [P, BT, NR * (P + HD)])
        kT, q_head = sb("kT", [P, N]), sb("q_head", [P, NR, N])
        q_late = sb("q_late", [P, BT, HALF])
        state = sb("state", [P, BT, P])
        energy = sb("energy", [P, 2, 2, 2 * NR, HALF])
        rot = energy[:].rearrange("p a k h n -> p (a k h n)")[:, 0:BT * 2 * P].rearrange("p (b n) -> p b n", b=BT)
        gate, gated = sb("gate", [P, N]), sb("gated", [P, N])
        x_bias = sb("x_bias", [P, BT, P])
        sums = sb("sums", [P, BT])
        pre1, x1 = sb("pre1", [P, BT, P]), sb("x1", [P, BT, P])
        ek, en = sb("ek", [P, BT, SEQ]), sb("en", [P, BT, SEQ])
        ekv, scan_a, scan_b = sb("ekv", [P, BT, SEQ]), sb("scan_a", [P, BT, SEQ]), sb("scan_b", [P, BT, SEQ])
        mix1, mix2, xo = sb("mix1", [P, BT, SEQ]), sb("mix2", [P, BT, SEQ]), sb("xo", [P, BT, SEQ])
        pre2 = sb("pre2", [P, BT, P])
        x2 = sb("x2", [P, 2, BT, P])
        xh, xl = sb("xh", [P, 2, N], F32R), sb("xl", [P, 2, N], F32R)
        logits, probs = sb("logits", [P, BT, NE]), sb("probs", [P, BT, NE])
        rest = sb("rest", [P, BT, NE])
        top8 = sb("top8", [P, BT, 8])
        norm8 = sb("norm8", [P, BT])
        parts = sb("parts", [P, BT, NG, 3, GE], BF16)
        combT = sb("combT", [3 * GE, 2, NG, N], BF16)
        carrier = sb("carrier", [P, 4])
        stats, mv = sb("stats", [P, BT, 6]), sb("mv", [P, BT, 2])
        nt = sb("nt", [P, 4, BT])

        act_s = sb("act_s", [P, 2, N])
        hw = sb("hw", [P, 3, N])
        hh, hl = sb("hh", [P, HSLOTS, N], F32R), sb("hl", [P, HSLOTS, N], F32R)
        y_out = sb("y_out", [P, BT, P])
        yT = gated
        ostats, omv, ont = sb("ostats", [P, BT, 6]), sb("omv", [P, BT, 2]), sb("ont", [P, 4, BT])

        ps_h = ctx.enter_context(nc.psum_tensor("ps_h", [P, 2, N], F32))
        ps_c = ctx.enter_context(nc.psum_tensor("ps_c", [P, 2, N], F32))
        ps_y = ctx.enter_context(nc.psum_tensor("ps_y", [P, N], F32))
        ps_f = ctx.enter_context(nc.psum_tensor("ps_f", [P, 3, N], F32))

        const_in, raw_in = sem("const_in"), [sem("raw_in0"), sem("raw_in1")]
        prep_mm, prep_step, exp_cols = sem("prep_mm"), sem("prep_step"), sem("exp_cols")
        prep_done, zeroed, carried, split_hi, split_done = sem("prep_done"), sem("zeroed"), sem("carried"), sem("split_hi"), sem("split_done")
        stored = [sem(f"stored{i}") for i in range(SLOTS)]
        x_in, x_bias_ready = sem("x_in"), sem("x_bias_ready")
        qkv_ready, silu_qk, v_copied = sem("qkv_ready"), sem("silu_qk"), sem("v_copied")
        gate_ready, gate_copied = sem("gate_ready"), sem("gate_copied")
        roped, kT_ready, kT_copied = sem("roped"), sem("kT_ready"), sem("kT_copied")
        qT_ready, q_act, q_dve = sem("qT_ready"), sem("q_act"), sem("q_dve")
        state_ready, state_masked = sem("state_ready"), sem("state_masked")
        energy_ready, energy_masked = sem("energy_ready"), sem("energy_masked")
        heads_done, gated_ready = sem("heads_done"), sem("gated_ready")
        proj_ready, squares, pre1_ready = sem("proj_ready"), sem("squares"), sem("pre1_ready")
        x1_ready, x1T_ready, exps = sem("x1_ready"), sem("x1T_ready"), sem("exps")
        xo_ready, xoT_ready, pre2_ready = sem("xo_ready"), sem("xoT_ready"), sem("pre2_ready")
        x2_ready, x2T_ready, xh_ready, xl_ready = sem("x2_ready"), sem("x2T_ready"), sem("xh_ready"), sem("xl_ready")
        logits_ready, biased, tanh_ready = sem("logits_ready"), sem("biased"), sem("tanh_ready")
        parts_ready, combT_ps, combT_ready = sem("parts_ready"), sem("combT_ps"), sem("combT_ready")
        dve_step = sem("dve_step")
        w_in = [sem(f"w_in{i}") for i in range(SLOTS)]
        h_ready, c_ready, act_ready, hw_ready = sem("h_ready"), sem("c_ready"), sem("act_ready"), sem("hw_ready")
        hh_ready, hl_ready, y_done = sem("hh_ready"), sem("hl_ready"), sem("y_done")
        y_copied, yT_ready, pre3_ready, out_ready, out_stored = (
            sem("y_copied"), sem("yT_ready"), sem("pre3_ready"), sem("out_ready"), sem("out_stored"))
        out_step = sem("out_step")

        block = ctx.enter_context(nc.Block())
        fixed = Tile(None, 0)

        def split_view(slot):
            return ring[:, slot].rearrange("p c (w h) n -> p c w h n", h=2)

        def ring_at(t, s, slots):
            return (t.par * STEPS + s) % slots

        def slot_words(slot):
            return ring[:, slot].bitcast(F32)

        @block.sync
        def _(sp):
            def load_tile(t):
                at = (lambda k: slice(t.base * k, (t.base + 1) * k)) if t.it is None else (
                    lambda k: bass.ds(t.at(k), k))
                sp.dma_start(xT_s[:], xT[:, at(N)]).then_inc(x_in, 16)
                sp.dma_start(xtok_s[:], xtok[:, at(BT), :]).then_inc(x_in, 16)
                sp.dma_start(cT_s[:], cT[:, at(BT), :]).then_inc(x_in, 16)

            def store_tile(t):
                sp.wait_ge(out_ready, t.at(1, 1))
                dst = out[:, t.base * BT:(t.base + 1) * BT, :] if t.it is None else out[:, bass.ds(t.at(BT), BT), :]
                sp.dma_start(dst, y_out[:]).then_inc(out_stored, 16)

            load_tile(fixed)
            consts = [(wqkv_s, wqkv), (wg1_s, wg1T), (wg2_s, wg2), (wo_s, wo), (cos_s, cosT), (sin_s, sinT),
                      (cmask_s, cmask), (bd_s, bdmask), (ident_s, ident), (hmask_s, hmask), (tm1_s, tm1),
                      (rw_f, rw), (rbias_s, rbias), (wgs_f, wgs), (wds_f, wds)]
            for dst, src in consts:
                sp.dma_start(dst[:], src).then_inc(const_in, 16)
            for i, src in enumerate([lnw, lnb, wx, ux]):
                sp.dma_start(cols[:, i:i + 1], src).then_inc(const_in, 16)
            sp.dma_start(wc_s[:, 1, :], center).then_inc(const_in, 16)
            sp.dma_start(q_head[0:3 * GE, :, :].rearrange("p a b -> p (a b)"), sel).then_inc(const_in, 16)

            def raw_chunk(c, src, dst, looped):
                if looped or c >= 2:
                    sp.wait_ge(split_done, split_count(c, looped, -1))
                sp.dma_start(raw[:, c % 2], src).then_inc(raw_in[c % 2], 16)
                if looped or c >= 1:
                    sp.wait_ge(split_done, split_count(c, looped, 0))
                    sp.dma_start(dst, slot_words((c - 1) % SLOTS)).then_inc(stored[(c - 1) % SLOTS], 16)

            def split_count(c, looped, more):
                return looped * SLOTS + (c + more) if looped else c + more

            for c in range(SLOTS):
                raw_chunk(c, experts[:, c * CH:(c + 1) * CH], scratch[:, (c - 1) * CH:c * CH] if c else None, 0)
            with sp.Fori(1, NCH // SLOTS) as i:
                for k in range(SLOTS):
                    sp.wait_ge(split_done, i * SLOTS + (k - 1))
                    sp.dma_start(raw[:, k % 2], experts[:, bass.ds(i * (SLOTS * CH) + k * CH, CH)]).then_inc(
                        raw_in[k % 2], 16)
                    sp.wait_ge(split_done, i * SLOTS + k)
                    sp.dma_start(scratch[:, bass.ds(i * (SLOTS * CH) + (k - 1) * CH, CH)],
                                 slot_words((k - 1) % SLOTS)).then_inc(stored[(k - 1) % SLOTS], 16)
            sp.wait_ge(split_done, NCH)
            sp.dma_start(scratch[:, (NCH - 1) * CH:NCH * CH], slot_words((NCH - 1) % SLOTS)).then_inc(
                stored[(NCH - 1) % SLOTS], 16)
            for k in range(SLOTS):
                sp.wait_ge(stored[k], 16 * (NCH // SLOTS))

            def experts_tile(t, last=False):
                if not last:
                    sp.wait_ge(xo_ready, t.at(1, 1))
                    load_tile(t.after(1))
                for c in range(NCH):
                    if c >= SLOTS:
                        sp.wait_ge(y_done, t.at(STEPS, CH * (c - SLOTS) + CH + 1))
                    else:
                        wait(sp, y_done, t.at(STEPS, CH * (NCH + c - SLOTS) + CH + 1 - STEPS)
                             if t.it is not None or t.base else 0)
                    sp.dma_start(slot_words(c % SLOTS), scratch[:, c * CH:(c + 1) * CH]).then_inc(w_in[c % SLOTS], 16)
                    if c == 7 and (t.it is not None or t.base):
                        store_tile(t.after(-1))

            experts_tile(fixed)
            with sp.Fori(0, LOOPS) as it:
                experts_tile(Tile(it, 1))
                experts_tile(Tile(it, 2))
            experts_tile(Tile(None, TILES - 1), last=True)
            store_tile(Tile(None, TILES - 1))
            sp.wait_ge(out_stored, 16 * TILES)

        @block.gpsimd
        def _(pool):
            pool.memset(v_head[:], 0.0).then_inc(zeroed, 1)
            for buf in (ekv, en, xo):
                pool.memset(buf[:, :, 0:1], 0.0).then_inc(zeroed, 1)

            def split(k, i, count):
                pool.wait_ge(raw_in[k % 2], (i * (SLOTS // 2) + (k // 2 + 1)) * 16)
                if not isinstance(i, int) or i > 0:
                    pool.wait_ge(stored[k], i * 16)
                pool.tensor_tensor(carrier[:, 2:3], raw[:, k % 2, 0, 0, 0:1], raw[:, k % 2, 0, 0, 0:1],
                                   ALU.add).then_inc(carried, 1)
                pool.tensor_copy(split_view(k)[:, :, :, 0, :], raw[:, k % 2]).then_inc(split_hi, 1)
                pool.wait_ge(split_hi, count)
                pool.tensor_tensor(split_view(k)[:, :, :, 1, :], raw[:, k % 2],
                                   split_view(k)[:, :, :, 0, :].bitcast(F32), ALU.subtract).then_inc(split_done, 1)

            def front(t):
                pool.wait_ge(x_in, t.at(48, 48))
                pool.tensor_tensor(x_bias[:], xtok_s[:], attn_bias[:].unsqueeze(1).to_broadcast([P, BT, P]),
                                   ALU.add).then_inc(x_bias_ready, 1)

            def experts_step(t, s):
                rows = INTER if s == 1 else P
                slot = ring_at(t, s - 1, HSLOTS)
                pool.wait_ge(hh_ready, t.at(STEPS, s))
                pool.tensor_tensor(hl[0:rows, slot], hw[0:rows, (s - 1) % 3], hh[0:rows, slot].bitcast(F32),
                                   ALU.subtract).then_inc(hl_ready, 1)

            def experts_tile(t, last=False):
                for s in range(1, STEPS + 1):
                    experts_step(t, s)
                    if s == 10 and not last:
                        front(t.after(1))

            pool.wait_ge(prep_done, 1)
            front(fixed)
            for k in range(SLOTS):
                split(k, 0, k + 1)
            with pool.Fori(1, NCH // SLOTS) as i:
                for k in range(SLOTS):
                    split(k, i, i * SLOTS + (k + 1))
            experts_tile(fixed)
            with pool.Fori(0, LOOPS) as it:
                experts_tile(Tile(it, 1))
                experts_tile(Tile(it, 2))
            experts_tile(Tile(None, TILES - 1), last=True)

        @block.scalar
        def _(act):
            def front(t, s):
                if s in PROJECT_AT:
                    b = PROJECT_AT.index(s)
                    act.wait_ge(qkv_ready, t.at(BT, b + 1))
                    act.activation(qk[:, b], ps_f[:, b % 2, 0:2 * P], ACT.Silu).then_inc(silu_qk, 1)
                if s == 13:
                    act.wait_ge(gate_ready, t.at(1, 1))
                    act.activation(gate[:], ps_f[:, 2], ACT.Tanh, scale=0.5).then_inc(gate_copied, 1)
                if s == 19:
                    act.wait_ge(kT_ready, t.at(1, 1))
                    act.activation(kT[:], ps_f[:, 0], ACT.Copy).then_inc(kT_copied, 1)
                    act.wait_ge(qT_ready, t.at(1, 1))
                    act.activation(q_head[:, 0], ps_f[:, 1], ACT.Identity, scale=hmask_s[:, 0:1]).then_inc(q_act, 1)
                if s == 20:
                    act.activation(q_head[:, 1], ps_f[:, 1], ACT.Identity, scale=hmask_s[:, 1:2]).then_inc(q_act, 1)
                    act.activation(q_late[:], ps_f[:, 1].rearrange("p (b n) -> p b n", b=BT)[:, :, HALF:SEQ],
                                   ACT.Copy).then_inc(q_act, 1)
                if s in (41, 42):
                    b0 = 2 * (s - 41)
                    act.wait_ge(proj_ready, t.at(2, s - 40))
                    for b in (b0, b0 + 1):
                        o = 2 * P * (b - b0) + P
                        act.activation(mix1[:, b], ps_f[:, b // 2, o:o + P], ACT.Square,
                                       accum_out=sums[:, b:b + 1]).then_inc(squares, 1)
                if s == 51:
                    act.wait_ge(x1T_ready, t.at(1, 1))
                    late = ps_f[:, 0].rearrange("p (b n) -> p b n", b=BT)[:, :, 1:SEQ]
                    act.activation(ek[:, :, 1:SEQ], late, ACT.Exp).then_inc(exps, 1)
                    act.activation(en[:, :, 1:SEQ], late, ACT.Exp, scale=-1.0).then_inc(exps, 1)
                if s == 67:
                    act.wait_ge(x2T_ready, t.at(1, 1))
                    act.activation(xh[:, t.par], ps_f[:, 0], ACT.Copy).then_inc(xh_ready, 1)
                if s == 71:
                    act.wait_ge(biased, t.at(1, 1))
                    act.activation(probs[:], logits[:], ACT.Tanh, scale=0.5).then_inc(tanh_ready, 1)
                if s == 80:
                  for i in range(3):
                    g0, g1 = 2 * i, min(2 * i + 2, NG)
                    act.wait_ge(combT_ps, t.at(3, i + 1))
                    act.activation(combT[:, t.par, g0:g1].rearrange("p g n -> p (g n)"),
                                   ps_f[:, (0, 2, 1)[i]].bitcast(BF16)[0:3 * GE, 0:(g1 - g0) * N],
                                   ACT.Copy).then_inc(combT_ready, 1)

            def experts_step(t, s):
                if s < STEPS:
                    rows = INTER if s == 0 else P
                    bank = (s + t.par) % 2
                    act.wait_ge(h_ready, t.at(STEPS, s + 1))
                    wait(act, hw_ready, t.at(STEPS, s - 1))
                    act.activation(act_s[0:rows, bank], ps_h[0:rows, bank], ACT.Silu).then_inc(act_ready, 1)
                if s >= 1:
                    rows = INTER if s == 1 else P
                    act.wait_ge(hw_ready, t.at(STEPS, s))
                    wait(act, y_done, t.at(STEPS, s - HSLOTS))
                    act.activation(hh[0:rows, ring_at(t, s - 1, HSLOTS)], hw[0:rows, (s - 1) % 3],
                                   ACT.Copy).then_inc(hh_ready, 1)

            def copy_y(t):
                act.wait_ge(y_done, t.at(STEPS, STEPS))
                act.activation(yT[:], ps_y[:], ACT.Copy).then_inc(y_copied, 1)

            def experts_tile(t, first=False, last=False):
                for s in range(STEPS + 1):
                    experts_step(t, s)
                    if s == LAG - 1 and not first:
                        copy_y(t.after(-1))
                    if not last:
                        front(t.after(1), s)

            act.wait_ge(const_in, 16 * NCONST)
            act.activation(cols[:, 4:5], cols[:, 2:3], ACT.Exp, scale=-1.0).then_inc(exp_cols, 1)
            act.activation(cols[:, 5:6], cols[:, 2:3], ACT.Exp).then_inc(exp_cols, 1)
            act.activation(cols[:, 6:7], cols[:, 3:4], ACT.Exp).then_inc(exp_cols, 1)
            for s in range(STEPS):
                front(fixed, s)
            experts_tile(fixed, first=True)
            with act.Fori(0, LOOPS) as it:
                experts_tile(Tile(it, 1))
                experts_tile(Tile(it, 2))
            experts_tile(Tile(None, TILES - 1), last=True)
            copy_y(Tile(None, TILES - 1))

        @block.vector
        def _(dve):
            steps = {}

            def link(ins, sem_, t=None, per_tile=0):
                steps[sem_] = steps.get(sem_, 0) + 1
                ins.then_inc(sem_, 1)
                dve.wait_ge(sem_, steps[sem_] if t is None else t.at(per_tile, steps[sem_]))

            def wide(ap, n):
                return ap.unsqueeze(2).to_broadcast([P, BT, n])

            def inverse_root(v, tmp, scale, lk, part):
                a, y, z = tmp[:, 0], tmp[:, 1], tmp[:, 2]
                if part == 0:
                    seed(v, a, y, z, scale, lk)
                for _ in range(1 + part):
                    lk(dve.scalar_tensor_tensor(out=z, in0=y, scalar=-0.5, in1=y, op0=ALU.mult, op1=ALU.mult))
                    lk(dve.tensor_tensor(z, z, a, ALU.mult))
                    lk(dve.scalar_tensor_tensor(out=y, in0=z, scalar=1.5, in1=y, op0=ALU.add, op1=ALU.mult))

            def seed(v, a, y, z, scale, lk):
                lk(dve.tensor_scalar(a, v, scale, EPS, ALU.mult, ALU.add))
                lk(dve.tensor_scalar(z.bitcast(I32), a.bitcast(I32), 1, None, ALU.logical_shift_right))
                lk(dve.tensor_scalar(y.bitcast(I32), z.bitcast(I32), -1, MAGIC, ALU.mult, ALU.add))

            def moments(src, st, m, lk):
                for b in range(BT):
                    last = dve.bn_stats(st[:, b], src[:, b])
                lk(last)
                dve.tensor_copy(carrier[:, 0:1], st[:, 0, 0:1])
                for b in range(BT):
                    last = dve.bn_aggr(m[:, b], st[:, b])
                lk(last)

            def normalise(dst, src, m, tmp):
                for b in range(BT):
                    last = dve.tensor_scalar(dst[:, b], src[:, b], m[:, b, 0:1], tmp[:, 1, b:b + 1],
                                             ALU.subtract, ALU.mult)
                return last

            def front(t, s):
                def lk(ins):
                    link(ins, dve_step, t, CHAIN)

                if s == 0:
                    steps[dve_step] = 0
                if s - 1 in PROJECT_AT:
                    b = PROJECT_AT.index(s - 1)
                    v = ps_f[:, b % 2, 2 * P:3 * P]
                    dve.wait_ge(silu_qk, t.at(BT, b + 1))
                    dve.tensor_copy(v_tok[:, b], v)
                    places = v_head[:, b].rearrange("p (r x) -> p r x", r=NR)[:, :, 0:P].rearrange(
                        "p r (j y) -> p r j y", j=NJ)[:, :, :, 0:HD]
                    dve.tensor_copy(places, v.rearrange("p (j r d) -> p r j d", j=NJ, r=NR)).then_inc(v_copied, 1)
                if s == 13:
                    dve.wait_ge(silu_qk, t.at(BT, BT))
                    lk(dve.tensor_tensor(qkr[:], qk[:], cos_s[:].unsqueeze(1).to_broadcast([P, BT, 2 * P]), ALU.mult))
                if s in (14, 15):
                    def halves(ap, h):
                        return ap.rearrange("p (g h d) -> p g h d", h=2, d=HD // 2)[:, :, h]
                    h = s - 14
                    src = qk[:].rearrange("p b (g h d) -> p b g h d", h=2, d=HD // 2)[:, :, :, 1 - h]
                    dst = rot.rearrange("p b (g h d) -> p b g h d", h=2, d=HD // 2)[:, :, :, h]
                    for b in range(BT):
                        last = dve.tensor_tensor(dst[:, b], src[:, b], halves(sin_s[:], h), ALU.mult)
                    lk(last)
                if s == 16:
                    dve.tensor_tensor(qkr[:], qkr[:], rot, ALU.add).then_inc(roped, 1)
                if s in (21, 22):
                    dve.wait_ge(q_act, t.at(3, 3))
                    r = s - 19
                    dve.tensor_scalar(q_head[:, r], ps_f[:, 1], hmask_s[:, r:r + 1], None, ALU.mult).then_inc(q_dve, 1)
                if s == 19:
                    dve.wait_ge(state_ready, t.at(1, 1))
                    dve.tensor_tensor(state[:], ps_f[:, 2].rearrange("p (b n) -> p b n", b=BT),
                                      bd_s[:].unsqueeze(1).to_broadcast([P, BT, P]), ALU.mult).then_inc(state_masked, 1)
                if s - 1 in ENERGY_AT or s - 2 in ENERGY_AT:
                    k = 0 if s - 1 in ENERGY_AT else 1
                    u = ENERGY_AT.index(s - 1 - k)
                    dve.wait_ge(energy_ready, t.at(8, 2 * u + k + 1))
                    if u == 2 and k == 0:
                        dve.wait_ge(heads_done, t.at(4, 2))
                    dve.tensor_tensor(energy[:, u % 2, k], ps_f[:, k].rearrange("p (h n) -> p h n", n=HALF),
                                      cmask_s[:].unsqueeze(1).to_broadcast([P, 8, HALF]),
                                      ALU.mult).then_inc(energy_masked, 1)
                if s == 39:
                    dve.wait_ge(heads_done, t.at(4, 4))
                    dve.wait_ge(gate_copied, t.at(1, 1))
                    dve.scalar_tensor_tensor(out=gated[:], in0=gate[:], scalar=1.0, in1=ps_f[:, 2],
                                             op0=ALU.add, op1=ALU.mult).then_inc(gated_ready, 1)
                if s == 43:
                    dve.wait_ge(squares, t.at(BT, BT))
                    inverse_root(sums[:], nt, 0.25 / P, lk, 0)
                if s == 44:
                    inverse_root(sums[:], nt, 0.25 / P, lk, 1)
                    lk(dve.tensor_scalar(nt[:, 3], nt[:, 1], 0.5, None, ALU.mult))
                if s == 45:
                    dve.wait_ge(x_bias_ready, t.at(1, 1))
                    for b in range(BT):
                        o = 2 * P * (b % 2)
                        last = dve.scalar_tensor_tensor(out=pre1[:, b], in0=ps_f[:, b // 2, o:o + P],
                                                        scalar=nt[:, 3, b:b + 1], in1=x_bias[:, b],
                                                        op0=ALU.mult, op1=ALU.add)
                    last.then_inc(pre1_ready, 1)
                    dve.wait_ge(pre1_ready, t.at(1, 1))
                if s == 46:
                    moments(pre1, stats, mv, lk)
                if s in (47, 48):
                    inverse_root(mv[:, :, 1], nt, 1.0, lk, s - 47)
                if s == 49:
                    normalise(x1, pre1, mv, nt).then_inc(x1_ready, 1)
                if s == 52:
                    dve.wait_ge(exps, t.at(2, 1))
                    lk(dve.tensor_tensor(ekv[:, :, 1:SEQ], ek[:, :, 1:SEQ], cT_s[:, :, 1:SEQ], ALU.mult))
                if s == 53:
                    dve.wait_ge(exps, t.at(2, 2))
                    flat = "p b n -> p (b n)"
                    dve.tensor_tensor_scan(scan_a[:].rearrange(flat), decay_a[:].rearrange(flat),
                                           ekv[:].rearrange(flat), 0.0, ALU.mult, ALU.add)
                    lk(dve.tensor_tensor_scan(scan_b[:].rearrange(flat), decay_b[:].rearrange(flat),
                                              en[:].rearrange(flat), 0.0, ALU.mult, ALU.add))
                now, before = slice(1, SEQ), slice(0, SEQ - 1)
                if s == 55:
                    lk(dve.tensor_tensor(mix1[:, :, now], cT_s[:, :, now], scan_b[:, :, before], ALU.mult))
                    lk(dve.tensor_tensor(mix1[:, :, now], mix1[:, :, now],
                                         tm1_s[:, now].unsqueeze(1).to_broadcast([P, BT, SEQ - 1]), ALU.add))
                if s == 56:
                    lk(dve.scalar_tensor_tensor(out=mix2[:, :, now], in0=ek[:, :, now], scalar=cols[:, 6:7],
                                                in1=mix1[:, :, now], op0=ALU.mult, op1=ALU.mult))
                    dve.tensor_tensor(xo[:, :, now], mix2[:, :, now], scan_a[:, :, before], ALU.add).then_inc(xo_ready, 1)
                if s == 60:
                    dve.wait_ge(xoT_ready, t.at(1, 1))
                    dve.tensor_tensor(pre2[:], x1[:], ps_f[:, 1].rearrange("p (b n) -> p b n", b=BT),
                                      ALU.add).then_inc(pre2_ready, 1)
                    dve.wait_ge(pre2_ready, t.at(1, 1))
                if s == 61:
                    moments(pre2, stats, mv, lk)
                if s in (62, 63):
                    inverse_root(mv[:, :, 1], nt, 1.0, lk, s - 62)
                if s == 64:
                    normalise(x2[:, t.par], pre2, mv, nt).then_inc(x2_ready, 1)
                if s == 68:
                    dve.wait_ge(xh_ready, t.at(1, 1))
                    dve.tensor_tensor(xl[:, t.par], ps_f[:, 0], xh[:, t.par].bitcast(F32),
                                      ALU.subtract).then_inc(xl_ready, 1)
                if s == 70:
                    dve.wait_ge(logits_ready, t.at(2, 2))
                    for k, bank in enumerate((1, 2)):
                        last = dve.tensor_tensor(logits[:, 2 * k:2 * k + 2],
                                                 ps_f[:, bank, 0:2 * NE].rearrange("p (b n) -> p b n", b=2),
                                                 rbias_s[:].unsqueeze(1).to_broadcast([P, 2, NE]), ALU.add)
                    last.then_inc(biased, 1)
                if s == 72:
                    dve.wait_ge(tanh_ready, t.at(1, 1))
                    dve.tensor_copy(carrier[:, 1:2], probs[:, 0, 0:1])
                    for b in range(BT):
                        last = dve.max(top8[:, b], probs[:, b])
                    lk(last)
                if s == 73:
                    for b in range(BT):
                        last = dve.match_replace(rest[:, b], top8[:, b], probs[:, b], -1.0)
                    lk(last)
                if s == 74:
                    dve.reduce_sum(norm8[:], top8[:], mybir.AxisListType.X)
                    lk(dve.tensor_tensor(probs[:], probs[:], rest[:], ALU.subtract))
                    lk(dve.tensor_scalar(norm8[:], norm8[:], 8.0 + 2e-9, 1 / 2.5, ALU.add, ALU.mult))
                    lk(dve.reciprocal(norm8[:], norm8[:]))
                if s == 75:
                    lk(dve.tensor_tensor(probs[:], probs[:], wide(norm8[:], NE), ALU.mult))
                by_group = probs[:].rearrange("p b (g e) -> p b g e", e=GE)
                if s == 76:
                    lk(dve.tensor_copy(parts[:, :, :, 0], by_group))
                    lk(dve.tensor_tensor(by_group, by_group, parts[:, :, :, 0], ALU.subtract))
                if s == 77:
                    lk(dve.tensor_copy(parts[:, :, :, 1], by_group))
                    lk(dve.tensor_tensor(by_group, by_group, parts[:, :, :, 1], ALU.subtract))
                if s == 78:
                    dve.tensor_copy(parts[:, :, :, 2], by_group).then_inc(parts_ready, 1)
                    assert steps[dve_step] == CHAIN, steps[dve_step]

            def experts_step(t, s):
                rows = INTER if s == 0 else P
                bank, slot = (s + t.par) % 2, s % 3
                dve.wait_ge(act_ready, t.at(STEPS, s + 1))
                wait(dve, hl_ready, t.at(STEPS, s - 2))
                if s == 0:
                    dve.tensor_copy(hw[0:rows, slot], act_s[0:rows, bank]).then_inc(hw_ready, 1)
                else:
                    dve.wait_ge(c_ready, t.at(PAIRS, s))
                    dve.tensor_tensor(hw[:, slot], act_s[:, bank], ps_c[:, bank], ALU.mult).then_inc(hw_ready, 1)

            def last_norm(t, s):
                def lk(ins):
                    link(ins, out_step, t, OUT_CHAIN)

                if s == 6:
                    steps[out_step] = 0
                    dve.wait_ge(yT_ready, t.at(1, 1))
                    wait(dve, out_stored, t.at(16))
                    dve.tensor_tensor(y_out[:], x2[:, t.par], ps_f[:, 0].rearrange("p (b n) -> p b n", b=BT),
                                      ALU.add).then_inc(pre3_ready, 1)
                    dve.wait_ge(pre3_ready, t.at(1, 1))
                if s == 7:
                    moments(y_out, ostats, omv, lk)
                if s in (9, 12):
                    inverse_root(omv[:, :, 1], ont, 1.0, lk, (s - 9) // 3)
                if s == 17:
                    normalise(y_out, y_out, omv, ont).then_inc(out_ready, 1)
                    assert steps[out_step] == OUT_CHAIN, steps[out_step]

            def experts_tile(t, first=False, last=False):
                for s in range(STEPS):
                    experts_step(t, s)
                    if not first:
                        last_norm(t.after(-1), s)
                    if not last:
                        front(t.after(1), s)

            def pk(ins):
                link(ins, prep_step)

            dve.wait_ge(const_in, 16 * NCONST)
            pk(dve.tensor_copy(identb[:], ident_s[:]))
            pk(dve.tensor_copy(sel_s[:], q_head[0:3 * GE].rearrange("p a b -> p (a b)").rearrange(
                "p (q n) -> p q n", q=16)))
            pk(dve.tensor_scalar(wow_s[:], wo_s[:], cols[:, 0:1], None, ALU.mult))
            pk(dve.tensor_scalar(lnb_wide[:], ident_s[:], 0.0, cols[:, 1:2], ALU.mult, ALU.add))
            for hi, lo, whole in ((rwh, rwl, rw_f), (wgsh, wgsl, wgs_f), (wdsh, wdsl, wds_f)):
                pk(dve.tensor_copy(hi[:], whole[:]))
                pk(dve.tensor_tensor(lo[:], whole[:], hi[:].bitcast(F32), ALU.subtract))
            pk(dve.memset(decay_a[:], 1.0))
            pk(dve.memset(decay_a[:, :, 0:1], 0.0))
            dve.wait_ge(exp_cols, 3)
            pk(dve.tensor_scalar(decay_b[:], decay_a[:], cols[:, 5:6], None, ALU.mult))
            pk(dve.tensor_scalar(decay_a[:], decay_a[:], cols[:, 4:5], None, ALU.mult))
            dve.wait_ge(prep_mm, 3)
            pk(dve.tensor_copy(wg_s[:], ps_f[:, 0, 0:P]))
            pk(dve.tensor_copy(wc_s[:, 0], ps_f[:, 1, 0:P]))
            dve.tensor_copy(attn_bias[:], ps_f[:, 2, 0:P]).then_inc(prep_done, 1)
            dve.wait_ge(prep_done, 1)
            dve.wait_ge(zeroed, 4)
            for s in range(STEPS):
                front(fixed, s)
            experts_tile(fixed, first=True)
            with dve.Fori(0, LOOPS) as it:
                experts_tile(Tile(it, 1))
                experts_tile(Tile(it, 2))
            t = Tile(None, TILES - 1)
            experts_tile(t, last=True)
            for s in range(STEPS):
                last_norm(t, s)

        @block.tensor
        def _(pe):
            def transposed(dst, src, ident_ap):
                return pe.transpose(dst, src, ident_ap)

            def three(dst, wh, wl, mh, ml, start, stop):
                pe.matmul(dst, wh, mh, start=start, stop=False, skip_group_check=True)
                pe.matmul(dst, wh, ml, start=False, stop=False, skip_group_check=True)
                return pe.matmul(dst, wl, mh, start=False, stop=stop, skip_group_check=True)

            def front(t, s):
                if s in PROJECT_AT:
                    b = PROJECT_AT.index(s)
                    if b == 0:
                        pe.wait_ge(x_in, t.at(48, 48))
                        wait(pe, combT_ready, t.at(3))
                    if b == 0 and (t.it is not None or t.base > 1):
                        pe.wait_ge(pre3_ready, t.at(1, -1))
                    if b >= 2:
                        pe.wait_ge(silu_qk, t.at(BT, b - 1))
                        pe.wait_ge(v_copied, t.at(BT, b - 1))
                    pe.matmul(ps_f[:, b % 2, 0:3 * P], xT_s[:, b * P:(b + 1) * P], wqkv_s[:],
                              start=True, stop=True).then_inc(qkv_ready, 1)
                if s == 12:
                    pe.matmul(ps_f[:, 2], wg_s[:], xT_s[:], start=True, stop=True).then_inc(gate_ready, 1)
                if s == 18:
                    pe.wait_ge(roped, t.at(1, 1))
                    for b in range(BT):
                        last = transposed(ps_f[:, 0, b * P:(b + 1) * P], qkr[:, b, P:2 * P], ident_s[:])
                    last.then_inc(kT_ready, 1)
                    pe.wait_ge(v_copied, t.at(BT, BT))
                    for b in range(BT):
                        last = transposed(ps_f[:, 1, b * P:(b + 1) * P], qkr[:, b, 0:P], ident_s[:])
                    last.then_inc(qT_ready, 1)
                    pe.wait_ge(gate_copied, t.at(1, 1))
                    for b in range(BT):
                        last = pe.matmul(ps_f[:, 2, b * P:(b + 1) * P], qkr[0:HALF, b, P:2 * P], v_tok[0:HALF, b],
                                         start=True, stop=True)
                    last.then_inc(state_ready, 1)
                if s in ENERGY_AT:
                    u = ENERGY_AT.index(s)
                    if u == 0:
                        pe.wait_ge(kT_copied, t.at(1, 1))
                        pe.wait_ge(q_dve, t.at(2, 2))
                        pe.wait_ge(state_masked, t.at(1, 1))
                    else:
                        pe.wait_ge(energy_masked, t.at(8, 2 * u))
                    for i in range(2):
                        for c in range(2):
                            n0 = (2 * (u // 2) + i) * SEQ + c * HALF
                            for k in range(2):
                                rows = slice(32 * (2 * (u % 2) + k), 32 * (2 * (u % 2) + k) + 32)
                                last = pe.matmul(
                                    ps_f[c * HALF:(c + 1) * HALF, k, i * 256:i * 256 + 256].rearrange(
                                        "p (r n) -> p r n", r=NR),
                                    kT[rows, n0:n0 + HALF], q_head[rows, :, n0:n0 + HALF],
                                    start=True, stop=True, skip_group_check=True)
                                if i == 1 and c == 1:
                                    last.then_inc(energy_ready, 1)
                if s in HEADS_AT or s - 1 in HEADS_AT:
                    c = int(s in HEADS_AT)
                    p = HEADS_AT.index(s if c else s - 1)
                    if c:
                        pe.wait_ge(energy_masked, t.at(8, 4 * p + 4))
                    toks = slice(c * HALF, (c + 1) * HALF)
                    for b in (2 * p, 2 * p + 1):
                        n0 = b * SEQ + c * HALF
                        if c:
                            pe.matmul(ps_f[:, 2, n0:n0 + HALF], state[:, b], q_late[:, b],
                                      start=True, stop=False, skip_group_check=True)
                        for r in range(NR):
                            for j in range(NJ):
                                last = pe.matmul(ps_f[32 * j:32 * j + 32, 2, n0:n0 + HALF],
                                                 v_head[toks, b, r * P + 32 * j:r * P + 32 * j + 32],
                                                 energy[toks, j // 2, j % 2, (b % 2) * NR + r],
                                                 start=(c == 0 and r == 0), stop=(r == NR - 1),
                                                 skip_group_check=True)
                    last.then_inc(heads_done, 1)
                    if c:
                        pe.wait_ge(heads_done, t.at(4, 2 * p + 1))
                if s in (40, 41):
                    k = s - 40
                    pe.wait_ge(gated_ready, t.at(1, 1))
                    for b in (2 * k, 2 * k + 1):
                        o = 2 * P * (b % 2)
                        last = pe.matmul(ps_f[:, k, o:o + 2 * P], gated[:, b * P:(b + 1) * P],
                                         wc_s[:].rearrange("p a n -> p (a n)"), start=True, stop=True)
                    last.then_inc(proj_ready, 1)
                if s == 50:
                    pe.wait_ge(x1_ready, t.at(1, 1))
                    for b in range(BT):
                        last = transposed(ps_f[:, 0, b * P:(b + 1) * P], x1[:, b], ident_s[:])
                    last.then_inc(x1T_ready, 1)
                if s == 59:
                    pe.wait_ge(xo_ready, t.at(1, 1))
                    for b in range(BT):
                        last = transposed(ps_f[:, 1, b * P:(b + 1) * P], xo[:, b], ident_s[:])
                    last.then_inc(xoT_ready, 1)
                if s == 66:
                    pe.wait_ge(x2_ready, t.at(1, 1))
                    for b in range(BT):
                        last = transposed(ps_f[:, 0, b * P:(b + 1) * P], x2[:, t.par, b], ident_s[:])
                    last.then_inc(x2T_ready, 1)
                if s == 69:
                    pe.wait_ge(xl_ready, t.at(1, 1))
                    for b in range(BT):
                        o = NE * (b % 2)
                        cols_ = slice(b * P, (b + 1) * P)
                        dst = ps_f[:, (1, 2)[b // 2], o:o + NE]
                        pe.matmul(dst, xh[:, t.par, cols_], rwh[:], start=True, stop=False)
                        pe.matmul(dst, xl[:, t.par, cols_], rwh[:], start=False, stop=False)
                        last = pe.matmul(dst, xh[:, t.par, cols_], rwl[:], start=False, stop=True)
                        if b % 2:
                            last.then_inc(logits_ready, 1)
                if s == 79:
                    pe.wait_ge(parts_ready, t.at(1, 1))
                    for g in range(NG):
                        for b in range(BT):
                            o = (g % 2) * N + b * P
                            last = transposed(ps_f[:, (0, 2, 1)[g // 2]].bitcast(BF16)[0:3 * GE, o:o + P],
                                              parts[:, b, g].rearrange("p a e -> p (a e)"), identb[:])
                        if g in (1, 3, 4):
                            last.then_inc(combT_ps, 1)

            def second_products(t, s):
                pe.wait_ge(hl_ready, t.at(STEPS, s + 1))
                slot = ring_at(t, s, HSLOTS)
                if s == 0:
                    wait(pe, y_copied, t.at(1))
                    three(ps_y[:], wdsh[:], wdsl[:], hh[0:INTER, slot], hl[0:INTER, slot],
                          True, False).then_inc(y_done, 1)
                else:
                    c, i = (s - 1) // CH, (s - 1) % CH
                    w = ring[:, c % SLOTS, i]
                    three(ps_y[:], w[:, 2], w[:, 3], hh[:, slot], hl[:, slot],
                          False, s == PAIRS).then_inc(y_done, 1)

            def first_products(t, s):
                bank = (s + t.par) % 2
                wait(pe, act_ready, t.at(STEPS, s - 1))
                if s == 0:
                    pe.wait_ge(xl_ready, t.at(1, 1))
                    three(ps_h[0:INTER, bank], wgsh[:], wgsl[:], xh[:, t.par], xl[:, t.par],
                          True, True).then_inc(h_ready, 1)
                    return
                c, i = (s - 1) // CH, (s - 1) % CH
                if i == 0:
                    pe.wait_ge(w_in[c % SLOTS], t.at(16 * (NCH // SLOTS), 16 * (c // SLOTS + 1)))
                w = ring[:, c % SLOTS, i]
                three(ps_h[:, bank], w[:, 0], w[:, 1], xh[:, t.par], xl[:, t.par], True, True).then_inc(h_ready, 1)

            def combine_rows(t, s):
                if s == 0:
                    return
                if s == 1:
                    pe.wait_ge(combT_ready, t.at(3, 3))
                wait(pe, hw_ready, t.at(STEPS, s - 1))
                g, q = (s - 1) // 16, (s - 1) % 16
                pe.matmul(ps_c[:, (s + t.par) % 2], sel_s[:, q], combT[:, t.par, g], start=True, stop=True).then_inc(c_ready, 1)

            def experts_tile(t, first=False, last=False):
                for s in range(STEPS):
                    first_products(t, s)
                    if s >= LAG:
                        second_products(t, s - LAG)
                    elif not first:
                        second_products(t.after(-1), STEPS + s - LAG)
                    combine_rows(t, s)
                    if s == LAG + 1 and not first:
                        turn_y(t.after(-1))
                    if not last:
                        front(t.after(1), s)

            def turn_y(t):
                pe.wait_ge(y_copied, t.at(1, 1))
                if t.it is not None or t.base != TILES - 1:
                    pe.wait_ge(combT_ready, t.at(3, 6))
                for b in range(BT):
                    last = transposed(ps_f[:, 0, b * P:(b + 1) * P], yT[:, b * P:(b + 1) * P], ident_s[:])
                last.then_inc(yT_ready, 1)

            pe.wait_ge(prep_step, 4)
            pe.matmul(ps_f[:, 0, 0:P], wg1_s[:], wg2_s[:], start=True, stop=True).then_inc(prep_mm, 1)
            pe.matmul(ps_f[:, 1, 0:P], wc_s[:, 1], wow_s[:], start=True, stop=True).then_inc(prep_mm, 1)
            pe.matmul(ps_f[:, 2, 0:P], lnb_wide[:], wo_s[:], start=True, stop=True).then_inc(prep_mm, 1)
            pe.wait_ge(prep_done, 1)
            for s in range(STEPS):
                front(fixed, s)
            experts_tile(fixed, first=True)
            with pe.Fori(0, LOOPS) as it:
                experts_tile(Tile(it, 1))
                experts_tile(Tile(it, 2))
            t = Tile(None, TILES - 1)
            experts_tile(t, last=True)
            for s in range(STEPS - LAG, STEPS):
                second_products(t, s)
            turn_y(t)


NCONST = 21


def kernel(x, ctx_1024, L0_attn_Wq, L0_attn_Wk, L0_attn_Wv, L0_attn_Wo, L0_attn_Wg1, L0_attn_Wg2, L0_attn_ln_w,
           L0_attn_ln_b, L0_xattn_w, L0_xattn_u, L0_ffn_router_w, L0_ffn_expert_bias, L0_ffn_w_gate, L0_ffn_w_down,
           L0_ffn_w_gate_shared, L0_ffn_w_down_shared):
    import concourse.bacc as bacc
    from concourse.bass_utils import run_bass_kernel_spmd

    a = {k: np.asarray(v) for k, v in dict(locals()).items() if k not in ("bacc", "run_bass_kernel_spmd")}
    x, ctx = a["x"], a["ctx_1024"]
    B = x.shape[0]

    pos = np.arange(SEQ, dtype=np.float32)
    freq = (np.float32(1.0) / np.float32(10000.0) ** (np.arange(0, HD, 2, dtype=np.float32) / np.float32(HD)))
    ang = pos[:, None] * freq.astype(np.float32)[None, :]
    cos, sin = np.cos(ang).astype(np.float32), np.sin(ang).astype(np.float32)
    heads = 2 * P // HD
    row = np.arange(P)
    tables = {
        "cosT": np.tile(np.concatenate([cos, cos], 1), (1, heads)),
        "sinT": np.tile(np.concatenate([-sin, sin], 1), (1, heads)),
        "cmask": ((row % HALF)[:, None] <= np.arange(HALF)[None, :]).astype(np.float32),
        "bdmask": (row[:, None] // HD == row[None, :] // HD).astype(np.float32),
        "ident": np.eye(P, dtype=np.float32),
        "center": (np.eye(P) - 1.0 / P).astype(np.float32),
        "hmask": ((row // HD % NR)[:, None] == np.arange(NR)[None, :]).astype(np.float32),
        "sel": (np.arange(3 * GE)[:, None, None] % GE == 2 * np.arange(16)[None, :, None] + row[None, None, :] // INTER
                ).astype(np.float32).reshape(3 * GE, 16 * P),
        "tm1": np.tile(np.maximum(np.arange(SEQ, dtype=np.float32) - 1, 0)[None, :], (P, 1)),
    }
    gate = a["L0_ffn_w_gate"].transpose(2, 0, 1).reshape(P, PAIRS, P)
    down = a["L0_ffn_w_down"].transpose(0, 2, 1).reshape(PAIRS, P, P).transpose(1, 0, 2)
    arrays = {
        "xT": x.reshape(-1, P).T, "xtok": x.transpose(1, 0, 2), "cT": ctx.transpose(2, 0, 1),
        "wqkv": np.concatenate([a["L0_attn_Wq"], a["L0_attn_Wk"], a["L0_attn_Wv"]], 1),
        "wg1T": a["L0_attn_Wg1"].T, "wg2": a["L0_attn_Wg2"], "wo": a["L0_attn_Wo"],
        "lnw": a["L0_attn_ln_w"][:, None], "lnb": a["L0_attn_ln_b"][:, None],
        "wx": a["L0_xattn_w"][:, None], "ux": a["L0_xattn_u"][:, None],
        "rw": a["L0_ffn_router_w"].T, "rbias": np.broadcast_to(a["L0_ffn_expert_bias"][None, :], (P, NE)),
        "wgs": a["L0_ffn_w_gate_shared"].T, "wds": a["L0_ffn_w_down_shared"].T,
        "experts": np.stack([gate, down], 2),
    } | tables
    nc = bacc.Bacc("TRN2", target_bir_lowering=False, num_devices=1)
    ins, maps = {}, {}
    for name, v in arrays.items():
        v = np.ascontiguousarray(v)
        maps[f"in_{name}"] = v
        ins[name] = nc.dram_tensor(f"in_{name}", v.shape, mybir.dt.from_np(v.dtype), kind="ExternalInput").ap()
    out = nc.dram_tensor("out", (SEQ, B, P), F32, kind="ExternalOutput").ap()
    build_program(nc, out=out, **ins)
    r = run_bass_kernel_spmd(nc, [maps], core_ids=[0])
    return r.results[0]["out"].transpose(1, 0, 2)
```

```python
from contextlib import ExitStack

import numpy as np
import concourse.bass as bass
from concourse import mybir

ALU = mybir.AluOpType
ACT = mybir.ActivationFunctionType
F32 = mybir.dt.float32
F32R = mybir.dt.float32r
BF16 = mybir.dt.bfloat16
I32 = mybir.dt.int32

P = 128
SEQ = 128
BT = 4
N = SEQ * BT
HALF = 64
HD = 8
NR, NJ = 4, 4
NE, INTER = 160, 64
PAIRS = NE // 2
STEPS = PAIRS + 1
LAG = 5
CH = 4
NCH = PAIRS // CH
SLOTS = 4
ROUNDS = NCH // SLOTS
GE = 32
NG = NE // GE
EPS = 1e-5
MAGIC = 0x5F3759DF
HSLOTS = 6
PROJECT_AT = (2, 3, 5, 6)
ENERGY_AT = (20, 23, 27, 30)
HEADS_AT = (26, 33)
GATE_AT, ROPE_AT, QKT_AT = 9, 9, 14
GATED_AT = 35
RMS_AT, PRE1_AT, X1_AT = 39, 42, 47
X1T_AT, MIX_AT, XOT_AT = 49, 51, 57
PRE2_AT, X2_AT, X2T_AT = 58, 63, 65
XL_AT, LOGITS_AT, TOP_AT, COMBT_AT = 67, 69, 72, 80
TURN_AT, PRE3_AT, STATS3_AT, OUT_AT = 6, 8, 13, 19
HIGH_AT = (21, 22, 23, 24)
SPLIT_LEAD = 7

CHAIN = 26
OUT_CHAIN = 4


class Tile:

    def __init__(self, it, base):
        self.it, self.base = it, base

    def at(self, k, more=0):
        if self.it is None:
            return self.base * k + more
        return self.it * (2 * k) + (self.base * k + more)

    def after(self, n):
        return Tile(self.it, self.base + n)

    @property
    def par(self):
        return self.base % 2


def wait(eng, sem, value):
    if not isinstance(value, int) or value > 0:
        eng.wait_ge(sem, value)


FIRST = (("ident", P), ("cols", 4), ("wo", P), ("center", P), ("wqkv", 3 * P))
REST = (("cos", 2 * P), ("sin", 2 * P), ("cmask", HALF), ("bdmask", P), ("hmask", NR), ("tm1", SEQ),
        ("rw", NE), ("rbias", NE), ("wgs", INTER))


def build_program(nc, xT, xtok, cT, first, later, wg12, wds, sel, experts, out):
    tokens = xT.shape[1]
    TILES = tokens // N
    LOOPS = (TILES - 2) // 2
    assert TILES == 2 * LOOPS + 2

    with ExitStack() as ctx:
        def sb(name, shape, dt=F32):
            return ctx.enter_context(nc.sbuf_tensor(name, shape, dt))

        def sem(name):
            return ctx.enter_context(nc.semaphore(name))

        scratch = nc.dram_tensor("split_experts", [P, PAIRS, 4, P], F32, kind="Internal").ap()

        first_s, later_s = sb("first_s", first.shape), sb("later_s", later.shape)
        views = {}
        for whole, fields in ((first_s, FIRST), (later_s, REST)):
            at = 0
            for name, width in fields:
                views[name] = whole[:, at:at + width]
                at += width
        wqkv_s, wo_s, ident_s, center_s = views["wqkv"], views["wo"], views["ident"], views["center"]
        cos_s, sin_s, cmask_s, bd_s = views["cos"], views["sin"], views["cmask"], views["bdmask"]
        hmask_s, tm1_s, rw_f, rbias_s, wgs_f = (
            views["hmask"], views["tm1"], views["rw"], views["rbias"], views["wgs"])
        ln_w, ln_b, w_col, u_col = (views["cols"][:, k:k + 1] for k in range(4))
        wg12_s = sb("wg12_s", [HD, 2, P])
        wg_s = sb("wg_s", [P, P])
        wow_s = sb("wow_s", [P, P])
        wc_s = sb("wc_s", [P, 2, P])
        lnb_wide, attn_bias = sb("lnb_wide", [P, P]), sb("attn_bias", [P, P])
        exp_s = sb("exp_s", [P, 3])
        identb = sb("identb", [P, P], BF16)
        sel_s = sb("sel_s", [3 * GE, 16, P], BF16)
        decay_a, decay_b = sb("decay_a", [P, BT, SEQ]), sb("decay_b", [P, BT, SEQ])
        rwh, rwl = sb("rwh", [P, NE], F32R), sb("rwl", [P, NE], F32R)
        wgsh, wgsl = sb("wgsh", [P, INTER], F32R), sb("wgsl", [P, INTER], F32R)
        wds_f, wdsh, wdsl = sb("wds_f", [INTER, P]), sb("wdsh", [INTER, P], F32R), sb("wdsl", [INTER, P], F32R)
        ring = sb("ring", [P, SLOTS, CH, 4, P], F32R)

        raw = sb("raw", [P, 2, CH, 2, P])

        xT_s, xtok_s, cT_s = sb("xT_s", [P, N]), sb("xtok_s", [P, BT, P]), sb("cT_s", [P, BT, SEQ])
        qk = sb("qk", [P, BT, 2 * P])
        qkr = sb("qkr", [P, BT, 2 * P])
        v_tok = sb("v_tok", [P, BT, P])
        v_head = sb("v_head", [P, BT, NR * (P + HD)])
        kT, q_head = sb("kT", [P, N]), sb("q_head", [P, NR, N])
        q_late = sb("q_late", [P, BT, HALF])
        state = sb("state", [P, BT, P])
        energy = sb("energy", [P, 2, 2, 2 * NR, HALF])
        rot = energy[:].rearrange("p a k h n -> p (a k h n)")[:, 0:BT * 2 * P].rearrange("p (b n) -> p b n", b=BT)
        gate, gated = sb("gate", [P, N]), sb("gated", [P, N])
        x_bias = sb("x_bias", [P, BT, P])
        sums = sb("sums", [P, BT])
        pre1, x1 = sb("pre1", [P, BT, P]), sb("x1", [P, BT, P])
        ek, en = sb("ek", [P, BT, SEQ]), sb("en", [P, BT, SEQ])
        ekv, scan_a, scan_b = sb("ekv", [P, BT, SEQ]), sb("scan_a", [P, BT, SEQ]), sb("scan_b", [P, BT, SEQ])
        mix1, mix2, xo = sb("mix1", [P, BT, SEQ]), sb("mix2", [P, BT, SEQ]), sb("xo", [P, BT, SEQ])
        pre2 = sb("pre2", [P, BT, P])
        x2 = sb("x2", [P, 2, BT, P])
        xh, xl = sb("xh", [P, 2, N], F32R), sb("xl", [P, 2, N], F32R)
        logits, probs = sb("logits", [P, BT, NE]), sb("probs", [P, BT, NE])
        rest = sb("rest", [P, BT, NE])
        top8 = sb("top8", [P, BT, 8])
        norm8 = sb("norm8", [P, BT])
        parts = sb("parts", [P, BT, NG, 3, GE], BF16)
        combT = sb("combT", [3 * GE, 2, NG, N], BF16)
        carrier = sb("carrier", [P, 4])
        stats, mv = sb("stats", [P, BT, 6]), sb("mv", [P, BT, 2])
        nt = sb("nt", [P, 4, BT])

        act_s = sb("act_s", [P, 2, N])
        hw = sb("hw", [P, 3, N])
        hh, hl = sb("hh", [P, HSLOTS, N], F32R), sb("hl", [P, HSLOTS, N], F32R)
        y_out = sb("y_out", [P, BT, P])
        yT = gated
        ostats, omv, ont = sb("ostats", [P, BT, 6]), sb("omv", [P, BT, 2]), sb("ont", [P, 4, BT])

        ps_h = ctx.enter_context(nc.psum_tensor("ps_h", [P, 2, N], F32))
        ps_c = ctx.enter_context(nc.psum_tensor("ps_c", [P, 2, N], F32))
        ps_y = ctx.enter_context(nc.psum_tensor("ps_y", [P, N], F32))
        ps_f = ctx.enter_context(nc.psum_tensor("ps_f", [P, 3, N], F32))

        first_in, const_in, raw_in = sem("first_in"), sem("const_in"), [sem("raw_in0"), sem("raw_in1")]
        prep_mm, prep_step, exp_cols = sem("prep_mm"), sem("prep_step"), sem("exp_cols")
        prep_done, zeroed, split_hi, low_begun, split_done = (
            sem("prep_done"), sem("zeroed"), sem("split_hi"), sem("low_begun"), sem("split_done"))
        stored = [sem(f"stored{i}") for i in range(SLOTS)]
        x_in, x_bias_ready = sem("x_in"), sem("x_bias_ready")
        qkv_ready, silu_qk, v_copied = sem("qkv_ready"), sem("silu_qk"), sem("v_copied")
        gate_ready, gate_copied = sem("gate_ready"), sem("gate_copied")
        roped, kT_ready, kT_copied = sem("roped"), sem("kT_ready"), sem("kT_copied")
        qT_ready, q_act, q_dve = sem("qT_ready"), sem("q_act"), sem("q_dve")
        state_ready, state_masked = sem("state_ready"), sem("state_masked")
        energy_ready, energy_masked = sem("energy_ready"), sem("energy_masked")
        heads_done, gated_ready = sem("heads_done"), sem("gated_ready")
        proj_ready, squares, pre1_ready = sem("proj_ready"), sem("squares"), sem("pre1_ready")
        x1_ready, x1T_ready, exps = sem("x1_ready"), sem("x1T_ready"), sem("exps")
        xo_ready, xoT_ready, pre2_ready = sem("xo_ready"), sem("xoT_ready"), sem("pre2_ready")
        x2_ready, x2T_ready, xh_ready, xl_ready = sem("x2_ready"), sem("x2T_ready"), sem("xh_ready"), sem("xl_ready")
        logits_ready, biased, tanh_ready = sem("logits_ready"), sem("biased"), sem("tanh_ready")
        parts_ready, combT_ps, combT_ready = sem("parts_ready"), sem("combT_ps"), sem("combT_ready")
        dve_step = sem("dve_step")
        w_in = [sem(f"w_in{i}") for i in range(SLOTS)]
        h_ready, c_ready, act_ready, hw_ready = sem("h_ready"), sem("c_ready"), sem("act_ready"), sem("hw_ready")
        hh_ready, hl_ready, y_done = sem("hh_ready"), sem("hl_ready"), sem("y_done")
        y_copied, yT_ready, pre3_ready, out_ready, out_stored = (
            sem("y_copied"), sem("yT_ready"), sem("pre3_ready"), sem("out_ready"), sem("out_stored"))
        out_step = sem("out_step")
        seeded, root_step, rooted = sem("seeded"), sem("root_step"), sem("rooted")
        out_seeded, out_root_step, out_rooted = sem("out_seeded"), sem("out_root_step"), sem("out_rooted")

        block = ctx.enter_context(nc.Block())
        fixed = Tile(None, 0)

        def split_view(slot):
            return ring[:, slot].rearrange("p c (w h) n -> p c w h n", h=2)

        def ring_at(t, s, slots):
            return (t.par * STEPS + s) % slots

        def slot_words(slot):
            return ring[:, slot].bitcast(F32)

        @block.sync
        def _(sp):
            def load_tile(t):
                at = (lambda k: slice(t.base * k, (t.base + 1) * k)) if t.it is None else (
                    lambda k: bass.ds(t.at(k), k))
                sp.dma_start(xT_s[:], xT[:, at(N)]).then_inc(x_in, 16)
                sp.dma_start(xtok_s[:], xtok[:, at(BT), :]).then_inc(x_in, 16)
                sp.dma_start(cT_s[:], cT[:, at(BT), :]).then_inc(x_in, 16)

            def load_next(t):
                sp.wait_ge(xo_ready, t.at(1, 1))
                load_tile(t.after(1))

            def store_tile(t):
                sp.wait_ge(out_ready, t.at(1, 1))
                dst = out[:, t.base * BT:(t.base + 1) * BT, :] if t.it is None else out[:, bass.ds(t.at(BT), BT), :]
                sp.dma_start(dst, y_out[:]).then_inc(out_stored, 16)

            sp.dma_start(first_s[:], first).then_inc(first_in, 16)
            sp.dma_start(wg12_s[:], wg12).then_inc(first_in, 16)
            load_tile(fixed)

            def load_raw(k, chunk):
                sp.dma_start(raw[:, k % 2], experts[:, chunk]).then_inc(raw_in[k % 2], 16)

            def pairs(i, k):
                if isinstance(i, int):
                    return slice((i * SLOTS + k) * CH, (i * SLOTS + k + 1) * CH)
                return bass.ds(i * (SLOTS * CH) + k * CH, CH)

            def pass_on(i, k, load=True):
                sp.wait_ge(split_done, i * SLOTS + (k + 1))
                if load:
                    load_raw(k, pairs(i, k + 2))
                sp.dma_start(scratch[:, pairs(i, k)], slot_words(k)).then_inc(stored[k], 16)

            for k in range(2):
                load_raw(k, pairs(0, k))
            sp.dma_start(later_s[:], later).then_inc(const_in, 16)
            sp.dma_start(wds_f[:], wds).then_inc(const_in, 16)
            sp.dma_start(q_head[0:3 * GE, :, :].rearrange("p a b -> p (a b)"), sel).then_inc(const_in, 16)
            for k in range(SLOTS):
                pass_on(0, k)
            load_next(fixed)
            with sp.Fori(1, ROUNDS - 1) as i:
                for k in range(SLOTS):
                    pass_on(i, k)
            for k in range(SLOTS):
                pass_on(ROUNDS - 1, k, load=k + 2 < SLOTS)
            for k in range(SLOTS):
                sp.wait_ge(stored[k], 16 * ROUNDS)

            def experts_tile(t, last=False):
                if not last:
                    load_next(t)
                for c in range(NCH):
                    if c >= SLOTS:
                        sp.wait_ge(y_done, t.at(STEPS, CH * (c - SLOTS) + CH + 1))
                    else:
                        sp.wait_ge(y_done, t.at(STEPS, CH * (NCH + c - SLOTS) + CH + 1 - STEPS))
                    sp.dma_start(slot_words(c % SLOTS), scratch[:, c * CH:(c + 1) * CH]).then_inc(w_in[c % SLOTS], 16)
                    if c == 7:
                        store_tile(t.after(-1))

            with sp.Fori(0, LOOPS) as it:
                experts_tile(Tile(it, 1))
                experts_tile(Tile(it, 2))
            experts_tile(Tile(None, TILES - 1), last=True)
            store_tile(Tile(None, TILES - 1))
            sp.wait_ge(out_stored, 16 * TILES)

        @block.gpsimd
        def _(pool):
            pool.memset(v_head[:], 0.0).then_inc(zeroed, 1)
            for buf in (ekv, en, xo):
                pool.memset(buf[:, :, 0:1], 0.0).then_inc(zeroed, 1)
            for tmp in (nt, ont):
                pool.memset(tmp[:, 3], 1.5).then_inc(zeroed, 1)
            pool.wait_ge(zeroed, 6)

            def low_half(q):
                k, some = q % SLOTS, slice(0 if q < SLOTS else CH // 2, CH)
                pool.wait_ge(split_hi, q + 1)
                if q >= SLOTS:
                    pool.wait_ge(low_begun, q + 1 - SLOTS)
                pool.tensor_tensor(split_view(k)[:, some, :, 1, :], raw[:, q % 2, some],
                                   split_view(k)[:, some, :, 0, :].bitcast(F32), ALU.subtract).then_inc(split_done, 1)

            steps = {}

            def newton(t, tmp, seeded, count, sem_, per_tile, done, part):
                a, y, z = tmp[:, 0], tmp[:, 1], tmp[:, 2]
                if part == 0:
                    pool.wait_ge(seeded, count)
                for i in range(6 * part, 6 * part + 6):
                    if i % 4 == 0:
                        last = pool.tensor_tensor(z, y, y, ALU.mult)
                    elif i % 4 == 1:
                        last = pool.tensor_tensor(z, z, a, ALU.mult)
                    elif i % 4 == 2:
                        last = pool.tensor_tensor(z, z, tmp[:, 3], ALU.add)
                    else:
                        last = pool.tensor_tensor(y, y, z, ALU.mult)
                    if i == 11:
                        last.then_inc(done, 1)
                    else:
                        steps[sem_] = steps.get(sem_, 0) + 1
                        last.then_inc(sem_, 1)
                        pool.wait_ge(sem_, t.at(per_tile, steps[sem_]))

            def roots(t, s):
                if s == 0:
                    steps[root_step] = 0
                for k, at in enumerate((RMS_AT, PRE1_AT + 2, PRE2_AT + 2)):
                    if s in (at, at + 1):
                        newton(t, nt, seeded, t.at(3, k + 1), root_step, 33, rooted, s - at)

            def last_root(t, s):
                if s == STATS3_AT + 1:
                    steps[out_root_step] = 0
                if s in (STATS3_AT + 1, STATS3_AT + 2):
                    newton(t, ont, out_seeded, t.at(1, 1), out_root_step, 11, out_rooted, s - STATS3_AT - 1)

            def front(t):
                pool.wait_ge(x_in, t.at(48, 48))
                pool.tensor_tensor(x_bias[:], xtok_s[:], attn_bias[:].unsqueeze(1).to_broadcast([P, BT, P]),
                                   ALU.add).then_inc(x_bias_ready, 1)

            def experts_step(t, s):
                rows = INTER if s == 1 else P
                slot = ring_at(t, s - 1, HSLOTS)
                pool.wait_ge(hh_ready, t.at(STEPS, s))
                pool.tensor_tensor(hl[0:rows, slot], hw[0:rows, (s - 1) % 3], hh[0:rows, slot].bitcast(F32),
                                   ALU.subtract).then_inc(hl_ready, 1)

            def experts_tile(t, first=False, last=False):
                for s in range(STEPS + 1):
                    c, odd = divmod(s + SPLIT_LEAD - 3, CH)
                    if first and not odd and SLOTS <= c < NCH:
                        low_half(c)
                    if s > 0:
                        experts_step(t, s)
                    if not first:
                        last_root(t.after(-1), s)
                    if not last:
                        if s == 10:
                            front(t.after(1))
                        roots(t.after(1), s)

            for s in range(STEPS):
                if s == 10:
                    pool.wait_ge(prep_done, 1)
                    front(fixed)
                if s in HIGH_AT:
                    low_half(HIGH_AT.index(s))
                roots(fixed, s)
            experts_tile(fixed, first=True)
            with pool.Fori(0, LOOPS) as it:
                experts_tile(Tile(it, 1))
                experts_tile(Tile(it, 2))
            experts_tile(Tile(None, TILES - 1), last=True)
            for s in range(STEPS):
                last_root(Tile(None, TILES - 1), s)

        @block.scalar
        def _(act):
            def front(t, s):
                if s in PROJECT_AT:
                    b = PROJECT_AT.index(s)
                    act.wait_ge(qkv_ready, t.at(BT, b + 1))
                    act.activation(qk[:, b], ps_f[:, 1 + b % 2, 0:2 * P], ACT.Silu).then_inc(silu_qk, 1)
                if s == GATE_AT + 1:
                    act.wait_ge(gate_ready, t.at(1, 1))
                    act.activation(gate[:], ps_f[:, 0], ACT.Tanh, scale=0.5).then_inc(gate_copied, 1)
                if s == QKT_AT + 1:
                    act.wait_ge(kT_ready, t.at(1, 1))
                    act.activation(kT[:], ps_f[:, 0], ACT.Copy).then_inc(kT_copied, 1)
                    act.wait_ge(qT_ready, t.at(1, 1))
                    act.activation(q_head[:, 0], ps_f[:, 1], ACT.Identity, scale=hmask_s[:, 0:1]).then_inc(q_act, 1)
                if s == QKT_AT + 2:
                    act.activation(q_head[:, 1], ps_f[:, 1], ACT.Identity, scale=hmask_s[:, 1:2]).then_inc(q_act, 1)
                    act.activation(q_late[:], ps_f[:, 1].rearrange("p (b n) -> p b n", b=BT)[:, :, HALF:SEQ],
                                   ACT.Copy).then_inc(q_act, 1)
                if s in (GATED_AT + 2, GATED_AT + 3):
                    b0 = 2 * (s - GATED_AT - 2)
                    act.wait_ge(proj_ready, t.at(2, s - GATED_AT - 1))
                    for b in (b0, b0 + 1):
                        o = 2 * P * (b - b0) + P
                        act.activation(mix1[:, b], ps_f[:, b // 2, o:o + P], ACT.Square,
                                       accum_out=sums[:, b:b + 1]).then_inc(squares, 1)
                if s == X1T_AT + 1:
                    act.wait_ge(x1T_ready, t.at(1, 1))
                    late = ps_f[:, 0].rearrange("p (b n) -> p b n", b=BT)[:, :, 1:SEQ]
                    act.activation(ek[:, :, 1:SEQ], late, ACT.Exp).then_inc(exps, 1)
                    act.activation(en[:, :, 1:SEQ], late, ACT.Exp, scale=-1.0).then_inc(exps, 1)
                if s == X2T_AT + 1:
                    act.wait_ge(x2T_ready, t.at(1, 1))
                    act.activation(xh[:, t.par], ps_f[:, 0], ACT.Copy).then_inc(xh_ready, 1)
                if s == LOGITS_AT + 2:
                    act.wait_ge(biased, t.at(1, 1))
                    act.activation(probs[:], logits[:], ACT.Tanh, scale=0.5).then_inc(tanh_ready, 1)
                if s == COMBT_AT:
                    for i in range(3):
                        g0, g1 = 2 * i, min(2 * i + 2, NG)
                        act.wait_ge(combT_ps, t.at(3, i + 1))
                        act.activation(combT[:, t.par, g0:g1].rearrange("p g n -> p (g n)"),
                                       ps_f[:, (0, 2, 1)[i]].bitcast(BF16)[0:3 * GE, 0:(g1 - g0) * N],
                                       ACT.Copy).then_inc(combT_ready, 1)

            def experts_step(t, s):
                if s < STEPS:
                    rows = INTER if s == 0 else P
                    bank = (s + t.par) % 2
                    act.wait_ge(h_ready, t.at(STEPS, s + 1))
                    wait(act, hw_ready, t.at(STEPS, s - 1))
                    act.activation(act_s[0:rows, bank], ps_h[0:rows, bank], ACT.Silu).then_inc(act_ready, 1)
                if s >= 1:
                    rows = INTER if s == 1 else P
                    act.wait_ge(hw_ready, t.at(STEPS, s))
                    wait(act, y_done, t.at(STEPS, s - HSLOTS))
                    act.activation(hh[0:rows, ring_at(t, s - 1, HSLOTS)], hw[0:rows, (s - 1) % 3],
                                   ACT.Copy).then_inc(hh_ready, 1)

            def copy_y(t):
                act.wait_ge(y_done, t.at(STEPS, STEPS))
                act.activation(yT[:], ps_y[:], ACT.Copy).then_inc(y_copied, 1)

            def high_half(q):
                k = q % SLOTS
                act.wait_ge(raw_in[q % 2], 16 * (q // 2 + 1))
                if q >= SLOTS:
                    act.wait_ge(stored[k], 16 * (q // SLOTS))
                    act.wait_ge(y_done, CH * (q - SLOTS) + CH + 1)
                act.activation(split_view(k)[:, :, :, 0, :], raw[:, q % 2], ACT.Copy).then_inc(split_hi, 1)

            def experts_tile(t, first=False, last=False):
                for s in range(STEPS + 1):
                    experts_step(t, s)
                    if first and (s + SPLIT_LEAD - 1) % CH == 0 and SLOTS <= (s + SPLIT_LEAD - 1) // CH < NCH:
                        high_half((s + SPLIT_LEAD - 1) // CH)
                    if s == LAG - 1 and not first:
                        copy_y(t.after(-1))
                    if not last:
                        front(t.after(1), s)

            act.wait_ge(first_in, 32)
            act.activation(exp_s[:, 0:1], w_col, ACT.Exp, scale=-1.0).then_inc(exp_cols, 1)
            act.activation(exp_s[:, 1:2], w_col, ACT.Exp).then_inc(exp_cols, 1)
            act.activation(exp_s[:, 2:3], u_col, ACT.Exp).then_inc(exp_cols, 1)
            for s in range(STEPS):
                if s in HIGH_AT:
                    high_half(HIGH_AT.index(s))
                if s == QKT_AT + 1:
                    act.wait_ge(const_in, 48)
                front(fixed, s)
            experts_tile(fixed, first=True)
            with act.Fori(0, LOOPS) as it:
                experts_tile(Tile(it, 1))
                experts_tile(Tile(it, 2))
            experts_tile(Tile(None, TILES - 1), last=True)
            copy_y(Tile(None, TILES - 1))

        @block.vector
        def _(dve):
            steps = {}

            def link(ins, sem_, t=None, per_tile=0, now=True):
                steps[sem_] = steps.get(sem_, 0) + 1
                ins.then_inc(sem_, 1)
                if now:
                    settle(sem_, t, per_tile)

            def settle(sem_, t=None, per_tile=0):
                dve.wait_ge(sem_, steps[sem_] if t is None else t.at(per_tile, steps[sem_]))

            def wide(ap, n):
                return ap.unsqueeze(2).to_broadcast([P, BT, n])

            def seed(v, tmp, scale, eps, lk, done):
                a, y, z = tmp[:, 0], tmp[:, 1], tmp[:, 2]
                lk(dve.tensor_scalar(a, v, scale, eps, ALU.mult, ALU.add))
                lk(dve.tensor_scalar(z.bitcast(I32), a.bitcast(I32), 1, None, ALU.logical_shift_right))
                dve.tensor_scalar(a, a, -0.5, None, ALU.mult)
                dve.tensor_scalar(y.bitcast(I32), z.bitcast(I32), -1, MAGIC, ALU.mult, ALU.add).then_inc(done, 1)

            def moments(src, st, m, lk, part):
                if part == 0:
                    for b in range(BT):
                        last = dve.bn_stats(st[:, b], src[:, b])
                    lk(last, now=False)
                else:
                    dve.tensor_copy(carrier[:, 0:1], st[:, 0, 0:1])
                    for b in range(BT):
                        last = dve.bn_aggr(m[:, b], st[:, b])
                    lk(last)

            def normalise(dst, src, m, tmp):
                for b in range(BT):
                    last = dve.tensor_scalar(dst[:, b], src[:, b], m[:, b, 0:1], tmp[:, 1, b:b + 1],
                                             ALU.subtract, ALU.mult)
                return last

            def front(t, s):
                def lk(ins, now=True):
                    link(ins, dve_step, t, CHAIN, now)

                def settled():
                    settle(dve_step, t, CHAIN)

                if s == 0:
                    steps[dve_step] = 0
                if s - 1 in PROJECT_AT:
                    b = PROJECT_AT.index(s - 1)
                    v = ps_f[:, 1 + b % 2, 2 * P:3 * P]
                    dve.wait_ge(silu_qk, t.at(BT, b + 1))
                    dve.tensor_copy(v_tok[:, b], v)
                    places = v_head[:, b].rearrange("p (r x) -> p r x", r=NR)[:, :, 0:P].rearrange(
                        "p r (j y) -> p r j y", j=NJ)[:, :, :, 0:HD]
                    dve.tensor_copy(places, v.rearrange("p (j r d) -> p r j d", j=NJ, r=NR)).then_inc(v_copied, 1)
                if s == ROPE_AT:
                    dve.wait_ge(silu_qk, t.at(BT, BT))
                    dve.tensor_tensor(qkr[:], qk[:], cos_s[:].unsqueeze(1).to_broadcast([P, BT, 2 * P]), ALU.mult)
                if s in (ROPE_AT + 1, ROPE_AT + 2):
                    def halves(ap, h):
                        return ap.rearrange("p (g h d) -> p g h d", h=2, d=HD // 2)[:, :, h]
                    h = s - ROPE_AT - 1
                    src = qk[:].rearrange("p b (g h d) -> p b g h d", h=2, d=HD // 2)[:, :, :, 1 - h]
                    dst = rot.rearrange("p b (g h d) -> p b g h d", h=2, d=HD // 2)[:, :, :, h]
                    for b in range(BT):
                        last = dve.tensor_tensor(dst[:, b], src[:, b], halves(sin_s[:], h), ALU.mult)
                    if h == 1:
                        lk(last, now=False)
                if s == ROPE_AT + 3:
                    settled()
                    dve.tensor_tensor(qkr[:], qkr[:], rot, ALU.add).then_inc(roped, 1)
                if s == QKT_AT + 1:
                    dve.wait_ge(state_ready, t.at(1, 1))
                    dve.tensor_tensor(state[:], ps_f[:, 2].rearrange("p (b n) -> p b n", b=BT),
                                      bd_s[:].unsqueeze(1).to_broadcast([P, BT, P]), ALU.mult).then_inc(state_masked, 1)
                if s in (QKT_AT + 3, QKT_AT + 4):
                    dve.wait_ge(q_act, t.at(3, 3))
                    r = s - QKT_AT - 1
                    dve.tensor_scalar(q_head[:, r], ps_f[:, 1], hmask_s[:, r:r + 1], None, ALU.mult).then_inc(q_dve, 1)
                if s - 1 in ENERGY_AT or s - 2 in ENERGY_AT:
                    k = 0 if s - 1 in ENERGY_AT else 1
                    u = ENERGY_AT.index(s - 1 - k)
                    dve.wait_ge(energy_ready, t.at(8, 2 * u + k + 1))
                    if u == 2 and k == 0:
                        dve.wait_ge(heads_done, t.at(4, 2))
                    dve.tensor_tensor(energy[:, u % 2, k], ps_f[:, k].rearrange("p (h n) -> p h n", n=HALF),
                                      cmask_s[:].unsqueeze(1).to_broadcast([P, 8, HALF]),
                                      ALU.mult).then_inc(energy_masked, 1)
                if s == GATED_AT:
                    dve.wait_ge(heads_done, t.at(4, 4))
                    dve.wait_ge(gate_copied, t.at(1, 1))
                    dve.scalar_tensor_tensor(out=gated[:], in0=gate[:], scalar=1.0, in1=ps_f[:, 2],
                                             op0=ALU.add, op1=ALU.mult).then_inc(gated_ready, 1)
                if s == RMS_AT:
                    dve.wait_ge(squares, t.at(BT, BT))
                    seed(sums[:], nt, 1.0 / P, 4 * EPS, lk, seeded)
                if s == PRE1_AT:
                    dve.wait_ge(rooted, t.at(3, 1))
                    dve.wait_ge(x_bias_ready, t.at(1, 1))
                    for b in range(BT):
                        o = 2 * P * (b % 2)
                        last = dve.scalar_tensor_tensor(out=pre1[:, b], in0=ps_f[:, b // 2, o:o + P],
                                                        scalar=nt[:, 1, b:b + 1], in1=x_bias[:, b],
                                                        op0=ALU.mult, op1=ALU.add)
                    last.then_inc(pre1_ready, 1)
                if s == PRE1_AT + 1:
                    dve.wait_ge(pre1_ready, t.at(1, 1))
                    dve.tensor_copy(carrier[:, 0:1], pre1[:, 0, 0:1])
                    moments(pre1, stats, mv, lk, 0)
                if s == PRE1_AT + 2:
                    settled()
                    moments(pre1, stats, mv, lk, 1)
                    seed(mv[:, :, 1], nt, 1.0, EPS, lk, seeded)
                if s == X1_AT:
                    dve.wait_ge(rooted, t.at(3, 2))
                    normalise(x1, pre1, mv, nt).then_inc(x1_ready, 1)
                if s == MIX_AT:
                    dve.wait_ge(exps, t.at(2, 1))
                    lk(dve.tensor_tensor(ekv[:, :, 1:SEQ], ek[:, :, 1:SEQ], cT_s[:, :, 1:SEQ], ALU.mult), now=False)
                if s == MIX_AT + 1:
                    settled()
                    dve.wait_ge(exps, t.at(2, 2))
                    flat = "p b n -> p (b n)"
                    dve.tensor_tensor_scan(scan_a[:].rearrange(flat), decay_a[:].rearrange(flat),
                                           ekv[:].rearrange(flat), 0.0, ALU.mult, ALU.add)
                    lk(dve.tensor_tensor_scan(scan_b[:].rearrange(flat), decay_b[:].rearrange(flat),
                                              en[:].rearrange(flat), 0.0, ALU.mult, ALU.add), now=False)
                now, before = slice(1, SEQ), slice(0, SEQ - 1)
                if s == MIX_AT + 3:
                    settled()
                    lk(dve.tensor_tensor(mix1[:, :, now], cT_s[:, :, now], scan_b[:, :, before], ALU.mult))
                    lk(dve.tensor_tensor(mix1[:, :, now], mix1[:, :, now],
                                         tm1_s[:, now].unsqueeze(1).to_broadcast([P, BT, SEQ - 1]), ALU.add), now=False)
                if s == MIX_AT + 4:
                    settled()
                    lk(dve.scalar_tensor_tensor(out=mix2[:, :, now], in0=ek[:, :, now], scalar=exp_s[:, 2:3],
                                                in1=mix1[:, :, now], op0=ALU.mult, op1=ALU.mult))
                    dve.tensor_tensor(xo[:, :, now], mix2[:, :, now], scan_a[:, :, before], ALU.add).then_inc(xo_ready, 1)
                if s == PRE2_AT:
                    dve.wait_ge(xoT_ready, t.at(1, 1))
                    dve.tensor_tensor(pre2[:], x1[:], ps_f[:, 1].rearrange("p (b n) -> p b n", b=BT),
                                      ALU.add).then_inc(pre2_ready, 1)
                if s == PRE2_AT + 1:
                    dve.wait_ge(pre2_ready, t.at(1, 1))
                    dve.tensor_copy(carrier[:, 0:1], pre2[:, 0, 0:1])
                    moments(pre2, stats, mv, lk, 0)
                if s == PRE2_AT + 2:
                    settled()
                    moments(pre2, stats, mv, lk, 1)
                    seed(mv[:, :, 1], nt, 1.0, EPS, lk, seeded)
                if s == X2_AT:
                    dve.wait_ge(rooted, t.at(3, 3))
                    normalise(x2[:, t.par], pre2, mv, nt).then_inc(x2_ready, 1)
                if s == XL_AT:
                    dve.wait_ge(xh_ready, t.at(1, 1))
                    dve.tensor_tensor(xl[:, t.par], ps_f[:, 0], xh[:, t.par].bitcast(F32),
                                      ALU.subtract).then_inc(xl_ready, 1)
                if s == LOGITS_AT + 1:
                    dve.wait_ge(logits_ready, t.at(2, 2))
                    for k, bank in enumerate((1, 2)):
                        last = dve.tensor_tensor(logits[:, 2 * k:2 * k + 2],
                                                 ps_f[:, bank, 0:2 * NE].rearrange("p (b n) -> p b n", b=2),
                                                 rbias_s[:].unsqueeze(1).to_broadcast([P, 2, NE]), ALU.add)
                    last.then_inc(biased, 1)
                if s == TOP_AT:
                    dve.wait_ge(tanh_ready, t.at(1, 1))
                    dve.tensor_copy(carrier[:, 1:2], probs[:, 0, 0:1])
                    for b in range(BT):
                        last = dve.max(top8[:, b], probs[:, b])
                    lk(last, now=False)
                if s == TOP_AT + 1:
                    settled()
                    dve.tensor_copy(carrier[:, 1:2], top8[:, 0, 0:1])
                    for b in range(BT):
                        last = dve.match_replace(rest[:, b], top8[:, b], probs[:, b], -1.0)
                    lk(last, now=False)
                if s == TOP_AT + 2:
                    settled()
                    dve.reduce_sum(norm8[:], top8[:], mybir.AxisListType.X)
                    lk(dve.tensor_tensor(probs[:], probs[:], rest[:], ALU.subtract))
                    lk(dve.tensor_scalar(norm8[:], norm8[:], 8.0 + 2e-9, 1 / 2.5, ALU.add, ALU.mult))
                    lk(dve.reciprocal(norm8[:], norm8[:]), now=False)
                if s == TOP_AT + 3:
                    settled()
                    lk(dve.tensor_tensor(probs[:], probs[:], wide(norm8[:], NE), ALU.mult), now=False)
                by_group = probs[:].rearrange("p b (g e) -> p b g e", e=GE)
                if s == TOP_AT + 4:
                    settled()
                    lk(dve.tensor_copy(parts[:, :, :, 0], by_group))
                    lk(dve.tensor_tensor(by_group, by_group, parts[:, :, :, 0], ALU.subtract), now=False)
                if s == TOP_AT + 5:
                    settled()
                    lk(dve.tensor_copy(parts[:, :, :, 1], by_group))
                    lk(dve.tensor_tensor(by_group, by_group, parts[:, :, :, 1], ALU.subtract), now=False)
                if s == TOP_AT + 6:
                    settled()
                    dve.tensor_copy(parts[:, :, :, 2], by_group).then_inc(parts_ready, 1)
                    assert steps[dve_step] == CHAIN, steps[dve_step]

            def experts_step(t, s):
                rows = INTER if s == 0 else P
                bank, slot = (s + t.par) % 2, s % 3
                dve.wait_ge(act_ready, t.at(STEPS, s + 1))
                wait(dve, hl_ready, t.at(STEPS, s - 2))
                if s == 0:
                    dve.tensor_copy(hw[0:rows, slot], act_s[0:rows, bank]).then_inc(hw_ready, 1)
                else:
                    dve.wait_ge(c_ready, t.at(PAIRS, s))
                    dve.tensor_tensor(hw[:, slot], act_s[:, bank], ps_c[:, bank], ALU.mult).then_inc(hw_ready, 1)

            def last_norm(t, s):
                def lk(ins, now=True):
                    link(ins, out_step, t, OUT_CHAIN, now)

                if s == PRE3_AT:
                    steps[out_step] = 0
                    dve.wait_ge(yT_ready, t.at(1, 1))
                    wait(dve, out_stored, t.at(16))
                    dve.tensor_tensor(y_out[:], x2[:, t.par], ps_f[:, 0].rearrange("p (b n) -> p b n", b=BT),
                                      ALU.add).then_inc(pre3_ready, 1)
                if s == STATS3_AT:
                    dve.wait_ge(pre3_ready, t.at(1, 1))
                    dve.tensor_copy(carrier[:, 2:3], y_out[:, 0, 0:1])
                    moments(y_out, ostats, omv, lk, 0)
                if s == STATS3_AT + 1:
                    settle(out_step, t, OUT_CHAIN)
                    moments(y_out, ostats, omv, lk, 1)
                    seed(omv[:, :, 1], ont, 1.0, EPS, lk, out_seeded)
                    assert steps[out_step] == OUT_CHAIN, steps[out_step]
                if s == OUT_AT:
                    dve.wait_ge(out_rooted, t.at(1, 1))
                    normalise(y_out, y_out, omv, ont).then_inc(out_ready, 1)

            def low_half(q):
                k, some = q % SLOTS, slice(0, CH // 2)
                dve.wait_ge(split_hi, q + 1)
                dve.tensor_tensor(split_view(k)[:, some, :, 1, :], raw[:, q % 2, some],
                                  split_view(k)[:, some, :, 0, :].bitcast(F32), ALU.subtract).then_inc(low_begun, 1)

            def experts_tile(t, first=False, last=False):
                for s in range(STEPS):
                    experts_step(t, s)
                    c, odd = divmod(s + SPLIT_LEAD - 2, CH)
                    if first and not odd and SLOTS <= c < NCH:
                        low_half(c)
                    if not first:
                        last_norm(t.after(-1), s)
                    if not last:
                        front(t.after(1), s)

            def pk(ins):
                link(ins, prep_step)

            def later_constants(s):
                if s == ROPE_AT - 1:
                    dve.wait_ge(const_in, 48)
                    pk(dve.tensor_copy(sel_s[:], q_head[0:3 * GE].rearrange("p a b -> p (a b)").rearrange(
                        "p (q n) -> p q n", q=16)))
                if s == PRE2_AT + 4:
                    for hi, lo, whole in ((rwh, rwl, rw_f), (wgsh, wgsl, wgs_f), (wdsh, wdsl, wds_f)):
                        pk(dve.tensor_copy(hi[:], whole[:]))
                        pk(dve.tensor_tensor(lo[:], whole[:], hi[:].bitcast(F32), ALU.subtract))
                if s == RMS_AT + 1:
                    pk(dve.memset(decay_a[:], 1.0))
                    pk(dve.memset(decay_a[:, :, 0:1], 0.0))
                    dve.wait_ge(exp_cols, 3)
                    pk(dve.tensor_scalar(decay_b[:], decay_a[:], exp_s[:, 1:2], None, ALU.mult))
                    pk(dve.tensor_scalar(decay_a[:], decay_a[:], exp_s[:, 0:1], None, ALU.mult))

            dve.wait_ge(first_in, 32)
            pk(dve.tensor_scalar(wow_s[:], wo_s, ln_w, None, ALU.mult))
            pk(dve.tensor_scalar(lnb_wide[:], ident_s, 0.0, ln_b, ALU.mult, ALU.add))
            pk(dve.tensor_copy(identb[:], ident_s))
            dve.wait_ge(prep_mm, 3)
            dve.tensor_copy(wg_s[:], ps_f[:, 0, 0:P])
            dve.tensor_copy(wc_s[:, 0], ps_f[:, 1, 0:P])
            dve.tensor_copy(wc_s[:, 1], center_s)
            dve.tensor_copy(attn_bias[:], ps_f[:, 2, 0:P]).then_inc(prep_done, 1)
            dve.wait_ge(prep_done, 1)
            dve.wait_ge(zeroed, 4)
            for s in range(STEPS):
                later_constants(s)
                front(fixed, s)
            experts_tile(fixed, first=True)
            with dve.Fori(0, LOOPS) as it:
                experts_tile(Tile(it, 1))
                experts_tile(Tile(it, 2))
            t = Tile(None, TILES - 1)
            experts_tile(t, last=True)
            for s in range(STEPS):
                last_norm(t, s)

        @block.tensor
        def _(pe):
            def transposed(dst, src, ident_ap):
                return pe.transpose(dst, src, ident_ap)

            def three(dst, wh, wl, mh, ml, start, stop):
                pe.matmul(dst, wh, mh, start=start, stop=False, skip_group_check=True)
                pe.matmul(dst, wh, ml, start=False, stop=False, skip_group_check=True)
                return pe.matmul(dst, wl, mh, start=False, stop=stop, skip_group_check=True)

            def front(t, s):
                if s in PROJECT_AT:
                    b = PROJECT_AT.index(s)
                    if b == 0:
                        pe.wait_ge(x_in, t.at(48, 48))
                        wait(pe, combT_ready, t.at(3))
                    if b >= 2:
                        pe.wait_ge(silu_qk, t.at(BT, b - 1))
                        pe.wait_ge(v_copied, t.at(BT, b - 1))
                    pe.matmul(ps_f[:, 1 + b % 2, 0:3 * P], xT_s[:, b * P:(b + 1) * P], wqkv_s[:],
                              start=True, stop=True).then_inc(qkv_ready, 1)
                if s == GATE_AT:
                    if t.it is not None or t.base > 1:
                        pe.wait_ge(pre3_ready, t.at(1, -1))
                    pe.matmul(ps_f[:, 0], wg_s[:], xT_s[:], start=True, stop=True).then_inc(gate_ready, 1)
                if s == QKT_AT:
                    pe.wait_ge(gate_copied, t.at(1, 1))
                    pe.wait_ge(roped, t.at(1, 1))
                    for b in range(BT):
                        last = transposed(ps_f[:, 0, b * P:(b + 1) * P], qkr[:, b, P:2 * P], ident_s[:])
                    last.then_inc(kT_ready, 1)
                    pe.wait_ge(v_copied, t.at(BT, BT))
                    for b in range(BT):
                        last = transposed(ps_f[:, 1, b * P:(b + 1) * P], qkr[:, b, 0:P], ident_s[:])
                    last.then_inc(qT_ready, 1)
                    for b in range(BT):
                        last = pe.matmul(ps_f[:, 2, b * P:(b + 1) * P], qkr[0:HALF, b, P:2 * P], v_tok[0:HALF, b],
                                         start=True, stop=True)
                    last.then_inc(state_ready, 1)
                if s in ENERGY_AT:
                    u = ENERGY_AT.index(s)
                    if u == 0:
                        pe.wait_ge(kT_copied, t.at(1, 1))
                        pe.wait_ge(q_dve, t.at(2, 2))
                        pe.wait_ge(state_masked, t.at(1, 1))
                    else:
                        pe.wait_ge(energy_masked, t.at(8, 2 * u))
                    for i in range(2):
                        for c in range(2):
                            n0 = (2 * (u // 2) + i) * SEQ + c * HALF
                            for k in range(2):
                                rows = slice(32 * (2 * (u % 2) + k), 32 * (2 * (u % 2) + k) + 32)
                                last = pe.matmul(
                                    ps_f[c * HALF:(c + 1) * HALF, k, i * 256:i * 256 + 256].rearrange(
                                        "p (r n) -> p r n", r=NR),
                                    kT[rows, n0:n0 + HALF], q_head[rows, :, n0:n0 + HALF],
                                    start=True, stop=True, skip_group_check=True)
                                if i == 1 and c == 1:
                                    last.then_inc(energy_ready, 1)
                if s in HEADS_AT or s - 1 in HEADS_AT:
                    c = int(s in HEADS_AT)
                    p = HEADS_AT.index(s if c else s - 1)
                    if c:
                        pe.wait_ge(energy_masked, t.at(8, 4 * p + 4))
                    toks = slice(c * HALF, (c + 1) * HALF)
                    for b in (2 * p, 2 * p + 1):
                        n0 = b * SEQ + c * HALF
                        if c:
                            pe.matmul(ps_f[:, 2, n0:n0 + HALF], state[:, b], q_late[:, b],
                                      start=True, stop=False, skip_group_check=True)
                        for r in range(NR):
                            for j in range(NJ):
                                last = pe.matmul(ps_f[32 * j:32 * j + 32, 2, n0:n0 + HALF],
                                                 v_head[toks, b, r * P + 32 * j:r * P + 32 * j + 32],
                                                 energy[toks, j // 2, j % 2, (b % 2) * NR + r],
                                                 start=(c == 0 and r == 0), stop=(r == NR - 1),
                                                 skip_group_check=True)
                    last.then_inc(heads_done, 1)
                    if c:
                        pe.wait_ge(heads_done, t.at(4, 2 * p + 1))
                if s in (GATED_AT + 1, GATED_AT + 2):
                    k = s - GATED_AT - 1
                    pe.wait_ge(gated_ready, t.at(1, 1))
                    for b in (2 * k, 2 * k + 1):
                        o = 2 * P * (b % 2)
                        last = pe.matmul(ps_f[:, k, o:o + 2 * P], gated[:, b * P:(b + 1) * P],
                                         wc_s[:].rearrange("p a n -> p (a n)"), start=True, stop=True)
                    last.then_inc(proj_ready, 1)
                if s == X1T_AT:
                    pe.wait_ge(x1_ready, t.at(1, 1))
                    for b in range(BT):
                        last = transposed(ps_f[:, 0, b * P:(b + 1) * P], x1[:, b], ident_s[:])
                    last.then_inc(x1T_ready, 1)
                if s == XOT_AT:
                    pe.wait_ge(xo_ready, t.at(1, 1))
                    for b in range(BT):
                        last = transposed(ps_f[:, 1, b * P:(b + 1) * P], xo[:, b], ident_s[:])
                    last.then_inc(xoT_ready, 1)
                if s == X2T_AT:
                    pe.wait_ge(x2_ready, t.at(1, 1))
                    for b in range(BT):
                        last = transposed(ps_f[:, 0, b * P:(b + 1) * P], x2[:, t.par, b], ident_s[:])
                    last.then_inc(x2T_ready, 1)
                if s == LOGITS_AT:
                    pe.wait_ge(xl_ready, t.at(1, 1))
                    for b in range(BT):
                        o = NE * (b % 2)
                        cols_ = slice(b * P, (b + 1) * P)
                        dst = ps_f[:, (1, 2)[b // 2], o:o + NE]
                        pe.matmul(dst, xh[:, t.par, cols_], rwh[:], start=True, stop=False)
                        pe.matmul(dst, xl[:, t.par, cols_], rwh[:], start=False, stop=False)
                        last = pe.matmul(dst, xh[:, t.par, cols_], rwl[:], start=False, stop=True)
                        if b % 2:
                            last.then_inc(logits_ready, 1)
                if s == COMBT_AT:
                    pe.wait_ge(parts_ready, t.at(1, 1))
                    for g in range(NG):
                        for b in range(BT):
                            o = (g % 2) * N + b * P
                            last = transposed(ps_f[:, (0, 2, 1)[g // 2]].bitcast(BF16)[0:3 * GE, o:o + P],
                                              parts[:, b, g].rearrange("p a e -> p (a e)"), identb[:])
                        if g in (1, 3, 4):
                            last.then_inc(combT_ps, 1)

            def second_products(t, s):
                pe.wait_ge(hl_ready, t.at(STEPS, s + 1))
                slot = ring_at(t, s, HSLOTS)
                if s == 0:
                    wait(pe, y_copied, t.at(1))
                    three(ps_y[:], wdsh[:], wdsl[:], hh[0:INTER, slot], hl[0:INTER, slot],
                          True, False).then_inc(y_done, 1)
                else:
                    c, i = (s - 1) // CH, (s - 1) % CH
                    w = ring[:, c % SLOTS, i]
                    three(ps_y[:], w[:, 2], w[:, 3], hh[:, slot], hl[:, slot],
                          False, s == PAIRS).then_inc(y_done, 1)

            def first_products(t, s, first):
                bank = (s + t.par) % 2
                wait(pe, act_ready, t.at(STEPS, s - 1))
                if s == 0:
                    pe.wait_ge(xl_ready, t.at(1, 1))
                    three(ps_h[0:INTER, bank], wgsh[:], wgsl[:], xh[:, t.par], xl[:, t.par],
                          True, True).then_inc(h_ready, 1)
                    return
                c, i = (s - 1) // CH, (s - 1) % CH
                if i == 0 and first:
                    pe.wait_ge(split_done, c + 1)
                elif i == 0:
                    pe.wait_ge(w_in[c % SLOTS], t.at(16 * ROUNDS, 16 * (c // SLOTS + 1 - ROUNDS)))
                w = ring[:, c % SLOTS, i]
                three(ps_h[:, bank], w[:, 0], w[:, 1], xh[:, t.par], xl[:, t.par], True, True).then_inc(h_ready, 1)

            def combine_rows(t, s):
                if s == 0:
                    return
                if s == 1:
                    pe.wait_ge(combT_ready, t.at(3, 3))
                wait(pe, hw_ready, t.at(STEPS, s - 1))
                g, q = (s - 1) // 16, (s - 1) % 16
                pe.matmul(ps_c[:, (s + t.par) % 2], sel_s[:, q], combT[:, t.par, g], start=True, stop=True).then_inc(c_ready, 1)

            def experts_tile(t, first=False, last=False):
                for s in range(STEPS):
                    first_products(t, s, first)
                    if s >= LAG:
                        second_products(t, s - LAG)
                    elif not first:
                        second_products(t.after(-1), STEPS + s - LAG)
                    combine_rows(t, s)
                    if s == TURN_AT and not first:
                        turn_y(t.after(-1))
                    if not last:
                        front(t.after(1), s)

            def turn_y(t):
                pe.wait_ge(y_copied, t.at(1, 1))
                if t.it is not None or t.base != TILES - 1:
                    pe.wait_ge(combT_ready, t.at(3, 6))
                for b in range(BT):
                    last = transposed(ps_f[:, 0, b * P:(b + 1) * P], yT[:, b * P:(b + 1) * P], ident_s[:])
                last.then_inc(yT_ready, 1)

            pe.wait_ge(prep_step, 2)
            pe.matmul(ps_f[:, 0, 0:P], wg12_s[:, 0], wg12_s[:, 1], start=True, stop=True).then_inc(prep_mm, 1)
            pe.matmul(ps_f[:, 1, 0:P], center_s, wow_s[:], start=True, stop=True).then_inc(prep_mm, 1)
            pe.matmul(ps_f[:, 2, 0:P], lnb_wide[:], wo_s[:], start=True, stop=True).then_inc(prep_mm, 1)
            pe.wait_ge(prep_done, 1)
            for s in range(STEPS):
                front(fixed, s)
            experts_tile(fixed, first=True)
            with pe.Fori(0, LOOPS) as it:
                experts_tile(Tile(it, 1))
                experts_tile(Tile(it, 2))
            t = Tile(None, TILES - 1)
            experts_tile(t, last=True)
            for s in range(STEPS - LAG, STEPS):
                second_products(t, s)
            turn_y(t)


def kernel(x, ctx_1024, L0_attn_Wq, L0_attn_Wk, L0_attn_Wv, L0_attn_Wo, L0_attn_Wg1, L0_attn_Wg2, L0_attn_ln_w,
           L0_attn_ln_b, L0_xattn_w, L0_xattn_u, L0_ffn_router_w, L0_ffn_expert_bias, L0_ffn_w_gate, L0_ffn_w_down,
           L0_ffn_w_gate_shared, L0_ffn_w_down_shared):
    import concourse.bacc as bacc
    from concourse.bass_utils import run_bass_kernel_spmd

    a = {k: np.asarray(v) for k, v in dict(locals()).items() if k not in ("bacc", "run_bass_kernel_spmd")}
    x, ctx = a["x"], a["ctx_1024"]
    B = x.shape[0]

    pos = np.arange(SEQ, dtype=np.float32)
    freq = (np.float32(1.0) / np.float32(10000.0) ** (np.arange(0, HD, 2, dtype=np.float32) / np.float32(HD)))
    ang = pos[:, None] * freq.astype(np.float32)[None, :]
    cos, sin = np.cos(ang).astype(np.float32), np.sin(ang).astype(np.float32)
    heads = 2 * P // HD
    row = np.arange(P)
    tables = {
        "cos": np.tile(np.concatenate([cos, cos], 1), (1, heads)),
        "sin": np.tile(np.concatenate([-sin, sin], 1), (1, heads)),
        "cmask": ((row % HALF)[:, None] <= np.arange(HALF)[None, :]).astype(np.float32),
        "bdmask": (row[:, None] // HD == row[None, :] // HD).astype(np.float32),
        "ident": np.eye(P, dtype=np.float32),
        "center": (np.eye(P) - 1.0 / P).astype(np.float32),
        "hmask": ((row // HD % NR)[:, None] == np.arange(NR)[None, :]).astype(np.float32),
        "tm1": np.tile(np.maximum(np.arange(SEQ, dtype=np.float32) - 1, 0)[None, :], (P, 1)),
    }
    sel = (np.arange(3 * GE)[:, None, None] % GE == 2 * np.arange(16)[None, :, None] + row[None, None, :] // INTER
           ).astype(np.float32).reshape(3 * GE, 16 * P)
    gate = a["L0_ffn_w_gate"].transpose(2, 0, 1).reshape(P, PAIRS, P)
    down = a["L0_ffn_w_down"].transpose(0, 2, 1).reshape(PAIRS, P, P).transpose(1, 0, 2)
    fields = {
        "cols": np.stack([a["L0_attn_ln_w"], a["L0_attn_ln_b"], a["L0_xattn_w"], a["L0_xattn_u"]], 1),
        "wo": a["L0_attn_Wo"], "wqkv": np.concatenate([a["L0_attn_Wq"], a["L0_attn_Wk"], a["L0_attn_Wv"]], 1),
        "rw": a["L0_ffn_router_w"].T, "rbias": np.broadcast_to(a["L0_ffn_expert_bias"][None, :], (P, NE)),
        "wgs": a["L0_ffn_w_gate_shared"].T,
    } | tables
    arrays = {
        "first": np.concatenate([fields[name] for name, _ in FIRST], 1),
        "later": np.concatenate([fields[name] for name, _ in REST], 1),
        "wg12": np.stack([a["L0_attn_Wg1"].T, a["L0_attn_Wg2"]], 1),
        "wds": a["L0_ffn_w_down_shared"].T, "sel": sel,
        "xT": x.reshape(-1, P).T, "xtok": x.transpose(1, 0, 2), "cT": ctx.transpose(2, 0, 1),
        "experts": np.stack([gate, down], 2),
    }
    nc = bacc.Bacc("TRN2", target_bir_lowering=False, num_devices=1)
    ins, maps = {}, {}
    for name, v in arrays.items():
        v = np.ascontiguousarray(v)
        maps[f"in_{name}"] = v
        ins[name] = nc.dram_tensor(f"in_{name}", v.shape, mybir.dt.from_np(v.dtype), kind="ExternalInput").ap()
    out = nc.dram_tensor("out", (SEQ, B, P), F32, kind="ExternalOutput").ap()
    build_program(nc, out=out, **ins)
    r = run_bass_kernel_spmd(nc, [maps], core_ids=[0])
    return r.results[0]["out"].transpose(1, 0, 2)
```
